# Optimizing a Trainium2 kernel written in Bass

```python
import numpy as np
import jax
import jax.numpy as jnp

def _softmax(x, axis=-1):
    return jax.nn.softmax(x, axis=axis)

def _gelu(x):
    return jax.nn.gelu(x, approximate=True)

def _silu(x):
    return jax.nn.silu(x)

def _sigmoid(x):
    return jax.nn.sigmoid(x)

def _layernorm(x, axis=-1, eps=1e-05):
    m = jnp.mean(x, axis=axis, keepdims=True)
    v = jnp.var(x, axis=axis, keepdims=True)
    return (x - m) / jnp.sqrt(v + eps)

def _scatter_add(tgt, idx, src, axis=0):
    return tgt.at[idx].add(src)

def _segment_sum(src, seg, n):
    return jax.ops.segment_sum(src, seg, n)
kernel_name = 'mk_gnn_resnorm_d1_gnn_r8_86e275'

def setup_inputs(seed: int=0):
    np.random.seed(seed)
    _w = jnp.asarray

    def _rec_inputs():
        import jax
        import jax.numpy as jnp
        _gk = jax.random.key(seed)
        x = -0.000202 + 1 * jax.random.normal(jax.random.fold_in(_gk, 1), (12500, 128), jnp.float32)
        src = jax.random.randint(jax.random.fold_in(_gk, 2), (200000,), 0, 12500, jnp.int32)
        dst = jnp.minimum((12500 * jax.random.uniform(jax.random.fold_in(_gk, 3), (200000,)) ** 2.0).astype(jnp.int32), 99999)
        _o = jnp.argsort(dst, stable=True)
        src = src[_o]
        dst = dst[_o]
        return (x, src, dst)
    x, src, dst = _rec_inputs()

    def _L0_gnn_setup():
        import jax, jax.numpy as jnp
        import numpy as np
        N_NODES = 6250
        N_EDGES = 100000
        IN_DIM = 128
        OUT_DIM = 128
        key = jax.random.key(seed)
        ks = jax.random.split(key, 8)
        x = jax.random.normal(ks[0], (N_NODES, IN_DIM), dtype=jnp.float32)
        edge_index = jax.random.randint(ks[1], (2, N_EDGES), 0, N_NODES, dtype=jnp.int64)
        s_in = 1.0 / np.sqrt(IN_DIM)
        s_up = 1.0 / np.sqrt(2 * OUT_DIM)
        W_lin = jax.random.uniform(ks[2], (IN_DIM, OUT_DIM), jnp.float32, -s_in, s_in)
        b_lin = jax.random.uniform(ks[3], (OUT_DIM,), jnp.float32, -s_in, s_in)
        W_msg = jax.random.uniform(ks[4], (IN_DIM, OUT_DIM), jnp.float32, -s_in, s_in)
        b_msg = jax.random.uniform(ks[5], (OUT_DIM,), jnp.float32, -s_in, s_in)
        W_upd = jax.random.uniform(ks[6], (2 * OUT_DIM, OUT_DIM), jnp.float32, -s_up, s_up)
        b_upd = jax.random.uniform(ks[7], (OUT_DIM,), jnp.float32, -s_up, s_up)
        return {'x': x, 'edge_index': edge_index, 'W_lin': W_lin, 'b_lin': b_lin, 'W_msg': W_msg, 'b_msg': b_msg, 'W_upd': W_upd, 'b_upd': b_upd}
    _L0_gnn_all = _L0_gnn_setup()
    _L0_gnn_in = {k: v for k, v in _L0_gnn_all.items() if k in ('W_lin', 'b_lin', 'W_msg', 'b_msg', 'W_upd', 'b_upd')}
    del _L0_gnn_all
    return {'x': x, 'src': src, 'dst': dst, 'L0_gnn_W_lin': _L0_gnn_in['W_lin'], 'L0_gnn_b_lin': _L0_gnn_in['b_lin'], 'L0_gnn_W_msg': _L0_gnn_in['W_msg'], 'L0_gnn_b_msg': _L0_gnn_in['b_msg'], 'L0_gnn_W_upd': _L0_gnn_in['W_upd'], 'L0_gnn_b_upd': _L0_gnn_in['b_upd']}

def reference(x, src, dst, L0_gnn_W_lin, L0_gnn_b_lin, L0_gnn_W_msg, L0_gnn_b_msg, L0_gnn_W_upd, L0_gnn_b_upd):
    import jax
    import jax.numpy as jnp

    def _L0_gnn_ref(x, edge_index, W_lin, b_lin, W_msg, b_msg, W_upd, b_upd):
        import jax, jax.numpy as jnp
        import numpy as np
        N_NODES = 6250
        N_EDGES = 100000
        IN_DIM = 128
        OUT_DIM = 128
        n_nodes = x.shape[0]
        row, col = (edge_index[0], edge_index[1])
        h_self = x @ W_lin + b_lin
        messages = x[col] @ W_msg + b_msg
        msg_sum = jax.ops.segment_sum(messages, row, num_segments=n_nodes)
        counts = jax.ops.segment_sum(jnp.ones((row.shape[0],), dtype=x.dtype), row, num_segments=n_nodes)
        h_agg = msg_sum / jnp.maximum(counts, 1.0)[:, None]
        h = jnp.concatenate([h_self, h_agg], axis=1) @ W_upd + b_upd
        return jax.nn.relu(h)
    edge_index = jnp.stack([src, dst])
    x = _layernorm(x + _L0_gnn_ref(x, edge_index, L0_gnn_W_lin, L0_gnn_b_lin, L0_gnn_W_msg, L0_gnn_b_msg, L0_gnn_W_upd, L0_gnn_b_upd), axis=-1)
    return x

_drawn_inputs = setup_inputs


def setup_inputs(seed=0):
    import zlib

    import numpy as np

    out = dict(_drawn_inputs(seed))
    spreads = {}
    factors = {'L0_gnn_b_lin': 3.778, 'L0_gnn_b_msg': 3.216}
    for name, (base, spread) in spreads.items():
        noise = np.random.default_rng([zlib.crc32(name.encode()), seed]).standard_normal(out[name].shape)
        drawn = base * np.exp(spread * noise) if base else spread * noise
        out[name] = jnp.asarray(drawn.astype(out[name].dtype))
    for name, factor in factors.items():
        out[name] = (out[name] * factor).astype(out[name].dtype)
    return out
```

```python
from contextlib import ExitStack

import numpy as np
import concourse.bass as bass
from concourse import mybir

P = 128


def gnn_program(nc, x, src, dst, w_lin, b_lin, w_msg, b_msg, w_upd, b_upd, out):
    f32, bf16, i32, u32 = mybir.dt.float32, mybir.dt.bfloat16, mybir.dt.int32, mybir.dt.uint32
    ALU, ACT, AX = mybir.AluOpType, mybir.ActivationFunctionType, mybir.AxisListType

    N, F = x.shape
    E = src.shape[0]
    TPG = 4
    GE = TPG * P
    GPR = 4
    RE = GPR * GE
    ROWS = -(-E // RE)
    FULL = E // RE
    REST = E - FULL * RE
    G = ROWS * GPR
    CPR = GPR * TPG
    NT = -(-N // P)
    NFULL = N // P
    NREST = N - NFULL * P
    assert NT == ROWS and ROWS < P
    NACC = TPG
    AR = N + P
    WS = GPR
    ZW = AR * F // P // 7
    assert ZW * 7 * P == AR * F
    TT = 7
    TG = NT // TT
    EPS = 1e-5

    acc = [nc.dram_tensor(f"sum{j}", [AR, F], f32, kind="Internal").ap() for j in range(NACC)]
    low_dram = nc.dram_tensor("window_low", [1, G], i32, kind="Internal").ap()

    ctx = ExitStack()
    with ctx:
        def sb(name, shape, dt):
            return ctx.enter_context(nc.sbuf_tensor(name, shape, dt))

        def ps(name, shape, dt=f32):
            return ctx.enter_context(nc.psum_tensor(name, shape, dt))

        def sem(name):
            return ctx.enter_context(nc.semaphore(name))

        x_sb = sb("x_sb", [P, NT, F], f32)
        base = sb("base", [P, NT, F], f32)
        flat = base[:, :, :].rearrange("p t f -> p (t f)")
        src_i = flat[0:ROWS, 0:RE].bitcast(i32)
        dst_i = flat[0:ROWS, RE:2 * RE].bitcast(i32)
        dst_f = flat[0:ROWS, 2 * RE:3 * RE]
        dst_rel = flat[0:ROWS, 3 * RE:4 * RE]
        src_hi_i = flat[0:ROWS, 4 * RE:5 * RE].bitcast(i32)
        src_lo_i = flat[0:ROWS, 5 * RE:6 * RE].bitcast(i32)
        src_hi = sb("src_hi", [ROWS, RE], bf16)
        src_lo = sb("src_lo", [ROWS, RE], bf16)
        col_src = sb("col_src", [P, ROWS, CPR], f32)
        col_key = sb("col_key", [P, ROWS, CPR], f32)
        col_dst = sb("col_dst", [P, ROWS, CPR], u32)
        col_hi = sb("col_hi", [P, ROWS, CPR], bf16)
        col_lo = sb("col_lo", [P, ROWS, CPR], bf16)

        low_f = sb("low_f", [ROWS, GPR], f32)
        high_f = sb("high_f", [ROWS, GPR], f32)
        low_i = sb("low_i", [ROWS, GPR], i32)
        wide4 = sb("wide4", [ROWS, GPR], f32)
        wide1 = sb("wide1", [ROWS, 1], f32)
        narrow_rows = sb("narrow_rows", [ROWS, 1], f32)
        low_used = sb("low_used", [ROWS, GPR], f32)
        wide = sb("wide", [P, 1], f32)
        narrow = sb("narrow", [P, 1], f32)
        wide_edge = sb("wide_edge", [P, 1], f32)
        wide_i = sb("wide_i", [1, 1], i32)

        iota_i = sb("iota_i", [P, P], i32)
        iota_f = sb("iota_f", [P, P], f32)
        edge_f = sb("edge_f", [P, 1], f32)
        trash = sb("trash", [P, TPG], f32)
        ident = sb("ident", [P, P], f32)
        ident_b = sb("ident_b", [P, P], bf16)
        ones = sb("ones", [P, P], f32)
        zeros_b = sb("zeros_b", [P, P], bf16)
        one_b = sb("one_b", [P, 1], bf16)

        w_lin_sb = sb("w_lin_sb", [P, F], f32)
        w_msg_sb = sb("w_msg_sb", [P, F], f32)
        wu_sb = sb("wu_sb", [P, 2, F], f32)
        w_linT = sb("w_linT", [P, P], f32)
        w_msgT = sb("w_msgT", [P, P], f32)
        A = sb("A", [P, F], f32)
        B = sb("B", [P, F], f32)
        b_lin_c = sb("b_lin_c", [P, 1], f32)
        b_msg_c = sb("b_msg_c", [P, 1], f32)
        b_msg_w = sb("b_msg_w", [P, P], f32)
        b_upd_r = sb("b_upd_r", [1, F], f32)
        const_row = sb("const_row", [1, F], f32)
        bmsg_rep = sb("bmsg_rep", [P, F], f32)

        win = sb("win", [P, WS, TPG, F], f32)
        eq = sb("eq", [P, 2, TPG, P], bf16)
        eq_before = sb("eq_before", [P, 2, TPG, P], bf16)
        hot_key = sb("hot_key", [P, 2, TPG, P], bf16)
        hot_lo = sb("hot_lo", [P, 2, TPG, P], bf16)
        hot_hi = sb("hot_hi", [P, 2, TPG, NT], bf16)
        M = sb("M", [P, 2, TPG, P], f32)
        rows = sb("rows", [P, GPR, TPG, F], f32)
        dup = sb("dup", [P, TPG], f32)
        idx = sb("idx", [P, GPR, TPG], u32)
        idx_x = sb("idx_x", [P, GPR, TPG], u32)
        zeros = rows[:, :, :, :].rearrange("p a b f -> p (a b f)")[:, 0:ZW]
        x_now = sb("x_now", [P, F], f32)
        xT = sb("xT", [P, P], f32)

        S = sb("S", [P, 2, NACC, TT, F], f32)
        inv = sb("inv", [P, NT], f32)
        some = sb("some", [P, NT], f32)
        cnt1 = sb("cnt1", [P, NT], f32)
        ST = M[:, 0, :, :]
        stats = sb("stats", [P, TT, 6], f32)
        mv = sb("mv", [P, TT, 2], f32)
        std = sb("std", [P, TT], f32)
        eps = sb("eps", [P, 1], f32)
        rstd = sb("rstd", [P, TT], f32)

        b_src = [ps(f"b_src{i}", [P, TPG, P]) for i in range(2)]
        b_M = ps("b_M", [P, TPG, P])
        b_rows = ps("b_rows", [P, TPG, F])
        b_hist = ps("b_hist", [P, 512])
        b_const = ps("b_const", [P, 512])
        b_dup = ps("b_dup", [P, 512])
        b_x = ps("b_x", [P, 4, P])
        hist = b_hist[:, 0:NT]
        c_iota = b_const[:, 0:P]
        c_before = b_const[:, P:2 * P]
        c_iota_hi = b_const[:, 2 * P:2 * P + NT]
        cols_ps = [b_src[0], b_src[1], b_M, b_rows, b_x]

        names = ("edges_loaded x_loaded weights_loaded zeros_set zeroed low_stored pads_set iota_set "
                 "consts_set rows_ready wide_summed wide_ready cols_made cols_taken wT_made wT_taken "
                 "w_made w_taken chain key_ready hist_zeroed "
                 "src_spread eq_ready before_ready key_hot lo_hot hi_hot M_made M_taken dup_made dup_taken "
                 "rows_made rows_taken idx_ready rows_free hist_made x_copied x_turned xT_taken base_made base_taken "
                 "pair_a pair_b S_summed S_turned ST_taken h_made z_ready y_ready gathering stats_ready aggregating mv_ready std_ready hist_final gather_idx").split()
        s = {n: sem("s_" + n) for n in names}
        win_loaded = [sem(f"s_win_loaded{i}") for i in range(WS)]
        win_gathered = [sem(f"s_win_gathered{i}") for i in range(WS)]
        added = [sem(f"s_added{j}") for j in range(NACC)]
        S_loaded = [sem(f"s_S_loaded{i}") for i in range(2)]

        stored = [sem(f"s_stored{i}") for i in range(2)]
        turned = [b_src[i][:, 0, :] for i in range(2)]
        h_ps = [b_M[:, 0, :], b_rows[:, 0, :]]

        def bc(a, n):
            return a.unsqueeze(2).to_broadcast([a.shape[0], a.shape[1], n])

        def rep(a, n):
            return a.unsqueeze(1).to_broadcast([a.shape[0], n, a.shape[1]])

        block = ctx.enter_context(nc.Block())

        @block.sync
        def _(sp):
            sp.wait_ge(s["pads_set"], 3)
            for part, lst in ((src_i, src), (dst_i, dst)):
                sp.dma_start(part[0:FULL, :], lst[0:FULL * RE].rearrange("(r f) -> r f", f=RE)).then_inc(s["edges_loaded"], 16)
                sp.dma_start(part[FULL:ROWS, 0:REST], lst[FULL * RE:E].rearrange("(r f) -> r f", r=1)).then_inc(s["edges_loaded"], 16)
            sp.dma_start(x_sb[0:NREST, NFULL, :], x[NFULL * P:N, :]).then_inc(s["x_loaded"], 16)
            sp.dma_start(x_sb[:, 0:NFULL, :], x[0:NFULL * P, :].rearrange("(t p) f -> p t f", p=P)).then_inc(s["x_loaded"], 16)
            sp.wait_ge(s["wide_ready"], 1)
            sp.dma_start(low_dram.rearrange("a (r g) -> (a r) g", g=GPR), low_i[:, :]).then_inc(s["low_stored"], 16)
            sp.wait_ge(s["low_stored"], 16)
            is_wide = sp.value_load(wide_i[0:1, 0:1], min_val=0, max_val=1)
            with sp.If(is_wide == 0):
                with sp.Fori(0, ROWS) as r:
                    for g in range(GPR):
                        low = sp.value_load(low_dram[0:1, bass.ds(r * GPR + g, 1)], min_val=0, max_val=N - P)
                        sp.wait_ge(s["rows_made"], r * GPR + g + 1)
                        sp.dma_start(win[:, g, 0, :], x[bass.ds(low, P), :]).then_inc(win_loaded[g], 16)
            for j in range(NACC):
                sp.wait_ge(added[j], 16 * G)
            def load_sums(t, b):
                    for j in range(NACC):
                        sp.dma_start(S[:, b, j, :, :], acc[j][bass.ds((t * 2 + b) * (TT * P), TT * P), :]
                                     .rearrange("(t p) f -> p t f", p=P)).then_inc(S_loaded[b], 16)
            load_sums(0, 0)
            load_sums(0, 1)
            with sp.Fori(1, TG // 2) as t:
                for b in range(2):
                    sp.wait_ge(stored[b], 16 * t)
                    load_sums(t, b)

        @block.scalar
        def _(act):
            act.dma_start(w_lin_sb[:, :], w_lin).then_inc(s["weights_loaded"], 16)
            act.dma_start(w_msg_sb[:, :], w_msg).then_inc(s["weights_loaded"], 16)
            act.dma_start(wu_sb[:, :, :], w_upd.rearrange("(a p) f -> p a f", p=P)).then_inc(s["weights_loaded"], 16)
            act.dma_start(b_lin_c[:, :], b_lin.rearrange("(p a) -> p a", a=1)).then_inc(s["weights_loaded"], 16)
            act.dma_start(b_msg_c[:, :], b_msg.rearrange("(p a) -> p a", a=1)).then_inc(s["weights_loaded"], 16)
            act.dma_start(b_upd_r[:, :], b_upd.rearrange("(a f) -> a f", a=1)).then_inc(s["weights_loaded"], 16)
            act.wait_ge(s["zeros_set"], 1)
            for j in range(NACC):
                act.dma_start(acc[j].rearrange("n f -> (n f)").rearrange("(p a w) -> p a w", a=7, w=ZW),
                              rep(zeros, 7)).then_inc(s["zeroed"], 16)
            act.wait_ge(s["wT_made"], 1)
            act.activation(w_linT[:, :], b_x[:, 0, :], ACT.Copy)
            act.activation(w_msgT[:, :], b_x[:, 1, :], ACT.Copy).then_inc(s["wT_taken"], 1)
            act.wait_ge(s["w_made"], 1)
            act.activation(A[:, :], b_x[:, 0, :], ACT.Copy)
            act.activation(B[:, :], b_x[:, 1, :], ACT.Copy)
            act.activation(bmsg_rep[:, :], b_x[:, 2, :], ACT.Copy)
            act.activation(const_row[:, :], b_x[0:1, 3, :], ACT.Copy).then_inc(s["w_taken"], 1)
            act.wait_ge(s["x_loaded"], 32)
            act.wait_ge(s["zeroed"], 16 * NACC)
            act.sem_inc(s["rows_taken"], 1)
            with act.Fori(0, ROWS) as r:
                for g in range(GPR):
                    i = r * GPR + g
                    act.wait_ge(s["M_made"], i + 1)
                    act.activation(M[:, g % 2, :, :], b_M[:, :, :], ACT.Copy).then_inc(s["M_taken"], 1)
                    act.wait_ge(s["rows_made"], i + WS + 1)
                    act.wait_ge(s["rows_free"], TPG * (i + 1))
                    act.activation(rows[:, g, :, :], b_rows[:, :, :], ACT.Copy).then_inc(s["rows_taken"], 1)
                    if g == 0:
                        act.activation(x_now[:, :], x_sb[:, bass.ds(r, 1), :].rearrange("p a f -> p (a f)"), ACT.Copy).then_inc(s["x_copied"], 1)
                    if g == 1:
                        act.wait_ge(s["x_turned"], r + 1)
                        act.activation(xT[:, :], b_x[:, 0, :], ACT.Copy).then_inc(s["xT_taken"], 1)
                    if g == 2:
                        act.wait_ge(s["base_made"], r + 1)
                        act.activation(base[:, bass.ds(r, 1), :], b_x[:, 1:2, :], ACT.Copy).then_inc(s["base_taken"], 1)
            def trip(t, b, last):
                i = t * 2 + b
                for k in range(TT):
                    act.wait_ge(s["S_turned"], i * TT + k + 1)
                    act.activation(ST[:, (b + k) % 2, :], turned[(b + k) % 2], ACT.Copy).then_inc(s["ST_taken"], 1)
                act.wait_ge(s["mv_ready"], i + 1)
                act.activation(std[:, :], mv[:, :, 1], ACT.Sqrt, bias=eps[:, :]).then_inc(s["std_ready"], 1)
                act.wait_ge(s["y_ready"], i + 1)
                whole = TT - 1 if last else TT
                act.dma_start(out[bass.ds(i * (TT * P), whole * P), :].rearrange("(t p) f -> p t f", p=P),
                              S[:, b, 3, 0:whole, :]).then_inc(stored[b], 16)
                if last:
                    act.dma_start(out[NFULL * P:N, :], S[0:NREST, b, 3, whole, :]).then_inc(stored[b], 16)

            with act.Fori(0, TG // 2 - 1) as t:
                for b in range(2):
                    trip(t, b, False)
            trip(TG // 2 - 1, 0, False)
            trip(TG // 2 - 1, 1, True)
            act.wait_ge(stored[0], 16 * (TG // 2))
            act.wait_ge(stored[1], 16 * (TG // 2 + 1))

        @block.gpsimd
        def _(pool):
            pool.iota(src_i.rearrange("r (k e) -> r k e", e=P), [[0, CPR], [1, P]], base=N, channel_multiplier=0).then_inc(s["pads_set"], 1)
            pool.iota(iota_i[:, :], [[1, P]], base=0, channel_multiplier=0).then_inc(s["iota_set"], 1)
            pool.memset(ident[:, :], 0.0).then_inc(s["consts_set"], 1)
            pool.memset(ones[:, :], 1.0).then_inc(s["consts_set"], 1)
            pool.wait_ge(s["consts_set"], 2)
            pool.affine_select(out=ident[:, :], in_=ident[:, :], compare_op=ALU.not_equal, fill=1.0, base=0,
                               pattern=[[-1, P]], channel_multiplier=1).then_inc(s["consts_set"], 1)
            pool.affine_select(out=xT[:, :], in_=ones[:, :], compare_op=ALU.is_gt, fill=0.0, base=0,
                               pattern=[[1, P]], channel_multiplier=-1).then_inc(s["consts_set"], 1)
            pool.wait_ge(s["wide_ready"], 1)
            is_wide = pool.value_load(wide_i[0:1, 0:1], min_val=0, max_val=1)
            pool.wait_ge(s["zeroed"], 16 * NACC)
            pool.sem_inc(s["rows_free"], 3 * TPG)

            def add_rows(i, g, first=False):
                pool.wait_ge(s["rows_taken"], i + 2)
                pool.wait_ge(s["idx_ready"], i + 1)
                for j in range(TPG):
                    if not first:
                        pool.wait_ge(added[j], 16 * i)
                    pool.sem_inc(s["rows_free"], 1)
                    pool.indirect_dma_start(out=acc[j], out_offset=bass.IndirectOffsetOnAxis(ap=idx[:, g, j:j + 1], axis=0),
                                            in_=rows[:, g, j, :], in_offset=None, compute_op=ALU.add).then_inc(added[j], 16)

            def gather_rows(i, g):
                pool.wait_ge(s["rows_made"], i + 1)
                pool.wait_ge(s["gather_idx"], i + 1)
                pool.sem_inc(s["gathering"], 1)
                for j in range(TPG):
                    pool.indirect_dma_start(out=win[:, g, j, :], out_offset=None, in_=x,
                                            in_offset=bass.IndirectOffsetOnAxis(ap=idx_x[:, g, j:j + 1], axis=0)
                                            ).then_inc(win_gathered[g], 16)

            with pool.If(is_wide == 0):
                for g in range(GPR):
                    add_rows(g, g, first=g == 0)
                with pool.Fori(1, ROWS) as r:
                    for g in range(GPR):
                        add_rows(r * GPR + g, g)
            with pool.Else():
                for g in range(GPR):
                    gather_rows(g, g)
                    add_rows(g, g, first=g == 0)
                with pool.Fori(1, ROWS) as r:
                    for g in range(GPR):
                        gather_rows(r * GPR + g, g)
                        add_rows(r * GPR + g, g)

            with pool.Fori(0, TG // 2) as t:
                for b in range(2):
                    pool.wait_ge(S_loaded[b], (t + 1) * 16 * NACC)
                    pool.tensor_tensor(S[:, b, 0, :, :], S[:, b, 0, :, :], S[:, b, 1, :, :], ALU.add).then_inc(s["pair_a"], 1)

        @block.vector
        def _(dve):
            links = [0]

            def link(ins):
                links[0] += 1
                ins.then_inc(s["chain"], 1)
                dve.wait_ge(s["chain"], links[0])

            nc.vector.memset(dst_i, N - 1).then_inc(s["pads_set"], 1)
            nc.vector.memset(zeros, 0.0).then_inc(s["zeros_set"], 1)
            nc.vector.memset(x_sb[:, NFULL, :], 0.0).then_inc(s["pads_set"], 1)
            nc.vector.memset(zeros_b[:, :], 0.0)
            nc.vector.memset(one_b[:, :], 1.0)
            nc.vector.memset(eps[:, :], EPS)
            dve.wait_ge(s["iota_set"], 1)
            link(nc.vector.tensor_copy(iota_f[:, :], iota_i[:, :]))
            link(nc.vector.tensor_copy(c_iota, iota_f[:, :]))
            link(nc.vector.tensor_scalar(c_iota_hi, iota_f[:, 0:NT], float(P), None, ALU.mult))
            dve.wait_ge(s["consts_set"], 4)
            link(nc.vector.tensor_copy(c_before, xT[:, :]))
            link(nc.vector.tensor_copy(ident_b[:, :], ident[:, :]))
            link(nc.vector.tensor_tensor(xT[:, :], ident[:, :], iota_f[:, :], ALU.mult))
            link(nc.vector.reduce_sum(edge_f[:, :], xT[:, :], AX.X))
            link(nc.vector.tensor_scalar(trash[:, :], edge_f[:, :].to_broadcast([P, TPG]), float(N), None, ALU.add))
            dve.wait_ge(s["edges_loaded"], 64)
            link(nc.vector.tensor_copy(dst_f, dst_i))
            d3 = dst_f.rearrange("r (g f) -> r g f", f=GE)
            link(nc.vector.tensor_reduce(high_f[:, :], d3, AX.X, ALU.max))
            link(nc.vector.tensor_reduce(low_f[:, :], d3, AX.X, ALU.min))
            link(nc.vector.tensor_scalar(low_f[:, :], low_f[:, :], float(N - P), None, ALU.min))
            link(nc.vector.tensor_copy(low_i[:, :], low_f[:, :]))
            link(nc.vector.tensor_tensor(high_f[:, :], high_f[:, :], low_f[:, :], ALU.subtract))
            link(nc.vector.tensor_scalar(wide4[:, :], high_f[:, :], P - 0.5, None, ALU.is_gt))
            nc.vector.reduce_max(wide1[:, :], wide4[:, :], AX.X).then_inc(s["rows_ready"], 1)
            dve.wait_ge(s["wide_summed"], 1)
            link(nc.vector.tensor_scalar(wide[:, :], b_x[:, 0, 0:1], 0.5, None, ALU.is_gt))
            nc.vector.tensor_copy(wide_i[:, :], wide[0:1, :]).then_inc(s["wide_ready"], 1)
            link(nc.vector.tensor_scalar(narrow[:, :], wide[:, :], -1.0, 1.0, ALU.mult, ALU.add))
            link(nc.vector.tensor_tensor(wide_edge[:, :], wide[:, :], edge_f[:, :], ALU.mult))
            link(nc.vector.tensor_scalar(low_used[:, :], low_f[:, :], narrow[0:ROWS, :], None, ALU.mult))
            nc.vector.tensor_tensor(dst_rel.rearrange("r (g f) -> r g f", f=GE), d3, bc(low_used[:, :], GE),
                                    ALU.subtract).then_inc(s["rows_ready"], 1)
            link(nc.vector.tensor_single_scalar(src_hi_i, src_i, 0x7FFFFF80, ALU.bitwise_and))
            link(nc.vector.tensor_single_scalar(src_lo_i, src_i, P - 1, ALU.bitwise_and))
            link(nc.vector.tensor_copy(src_hi[:, :], src_hi_i))
            nc.vector.tensor_copy(src_lo[:, :], src_lo_i).then_inc(s["rows_ready"], 1)
            dve.wait_ge(s["weights_loaded"], 96)
            nc.vector.tensor_copy(b_msg_w[:, :], b_msg_c[:, :].to_broadcast([P, P])).then_inc(s["rows_ready"], 1)
            for g in range(GPR):
                dve.wait_ge(s["cols_made"], g + 1)
                for k, to in enumerate((col_src, col_hi, col_lo, col_key, col_dst)):
                    last = nc.vector.tensor_copy(
                        to[:, :, g * TPG:(g + 1) * TPG].rearrange("p r j -> p j r"),
                        cols_ps[k][:, :, 0:ROWS])
                last.then_inc(s["cols_taken"], 1)
            dve.wait_ge(s["cols_taken"], GPR)
            nc.vector.tensor_scalar(col_key[:, :, :], col_key[:, :, :], narrow[:, :], wide_edge[:, :], ALU.mult,
                                    ALU.add).then_inc(s["key_ready"], 1)
            dve.wait_ge(s["key_ready"], 1)
            dve.wait_ge(s["zeroed"], 16 * NACC)
            dve.sem_inc(s["dup_taken"], 1)

            with dve.Fori(0, ROWS) as r:
                for g in range(GPR):
                    i = r * GPR + g
                    cols = slice(g * TPG, (g + 1) * TPG)

                    def col(a):
                        return a[:, bass.ds(r, 1), cols].rearrange("p a k -> p (a k)")
                    b = g % 2
                    dve.wait_ge(s["src_spread"], i + 1)
                    nc.vector.tensor_tensor(eq[:, b, :, :], b_src[b][:, :, :], bc(col(col_src), P), ALU.is_equal).then_inc(s["eq_ready"], 1)
                    nc.vector.tensor_tensor(hot_key[:, b, :, :], rep(c_iota, TPG), bc(col(col_key), P), ALU.is_equal).then_inc(s["key_hot"], 1)
                    dve.wait_ge(s["eq_ready"], i + 1)
                    nc.vector.tensor_tensor(eq_before[:, b, :, :], rep(c_before, TPG), eq[:, b, :, :], ALU.mult).then_inc(s["before_ready"], 1)
                    dve.wait_ge(s["rows_free"], TPG * (i + 1))
                    nc.vector.tensor_copy(idx_x[:, g, :], col(col_dst)).then_inc(s["gather_idx"], 1)
                    nc.vector.tensor_tensor(hot_lo[:, b, :, :], rep(c_iota, TPG), bc(col(col_lo), P), ALU.is_equal).then_inc(s["lo_hot"], 1)
                    nc.vector.tensor_tensor(hot_hi[:, b, :, :], rep(c_iota_hi, TPG), bc(col(col_hi), NT), ALU.is_equal).then_inc(s["hi_hot"], 1)
                    dve.wait_ge(s["dup_made"], i + 1)
                    nc.vector.scalar_tensor_tensor(out=dup[:, :], in0=b_dup[:, 0:TPG], scalar=1.0, in1=trash[:, :],
                                                   op0=ALU.min, op1=ALU.mult).then_inc(s["dup_taken"], 1)
                    dve.wait_ge(s["dup_taken"], i + 2)
                    nc.vector.tensor_tensor(idx[:, g, :], dup[:, :], col(col_src), ALU.max).then_inc(s["idx_ready"], 1)

            dve.wait_ge(s["hist_final"], 1)
            link(nc.vector.tensor_scalar(some[:, :], hist, 1.0, None, ALU.min))
            link(nc.vector.tensor_scalar(cnt1[:, :], hist, 1.0, None, ALU.max))
            link(nc.vector.reciprocal(inv[:, :], cnt1[:, :]))
            dve.sem_inc(s["z_ready"], 2)
            dve.wait_ge(s["base_taken"], ROWS)
            with dve.Fori(0, TG // 2) as t:
                for b in range(2):
                    i = t * 2 + b
                    own = [0]

                    def step(ins):
                        own[0] += 1
                        ins.then_inc(s["pair_b"], 1)
                        dve.wait_ge(s["pair_b"], t * (2 * STEPS) + b * STEPS + own[0])
                    STEPS = 4
                    dve.wait_ge(S_loaded[b], (t + 1) * 16 * NACC)
                    step(nc.vector.tensor_tensor(S[:, b, 2, :, :], S[:, b, 2, :, :], S[:, b, 3, :, :], ALU.add))
                    dve.wait_ge(s["pair_a"], i + 1)
                    nc.vector.tensor_tensor(S[:, b, 0, :, :], S[:, b, 0, :, :], S[:, b, 2, :, :], ALU.add).then_inc(s["S_summed"], 1)
                    Z = S[:, b, 1, :, :]
                    Y = S[:, b, 3, :, :]
                    for k in range(TT):
                        n = i * TT + k
                        last = nc.vector.scalar_tensor_tensor(
                            out=Z[:, k, :], in0=bmsg_rep[:, :], scalar=some[:, bass.ds(n, 1)],
                            in1=base[:, bass.ds(n, 1), :].rearrange("p a f -> p (a f)"), op0=ALU.mult, op1=ALU.add)
                    step(last)
                    for k in range(TT):
                        n = i * TT + k
                        dve.wait_ge(s["h_made"], n + 1)
                        last = nc.vector.scalar_tensor_tensor(
                            out=Y[:, k, :], in0=h_ps[(b + k) % 2], scalar=inv[:, bass.ds(n, 1)],
                            in1=Z[:, k, :], op0=ALU.mult, op1=ALU.add)
                        last.then_inc(s["z_ready"], 1)
                    dve.wait_ge(s["z_ready"], (i + 1) * TT + 2)
                    step(nc.vector.scalar_tensor_tensor(out=Z, in0=Y, scalar=0.0, in1=x_sb[:, bass.ds(i * TT, TT), :],
                                                        op0=ALU.max, op1=ALU.add))
                    for k in range(TT):
                        last = nc.vector.bn_stats(stats[:, k, :], Z[:, k, :])
                    last.then_inc(s["stats_ready"], 1)
                    dve.wait_ge(s["stats_ready"], i + 1)
                    dve.sem_inc(s["aggregating"], 1)
                    for k in range(TT):
                        last = nc.vector.bn_aggr(mv[:, k, :], stats[:, k, :])
                    last.then_inc(s["mv_ready"], 1)
                    dve.wait_ge(s["std_ready"], i + 1)
                    step(nc.vector.reciprocal(rstd[:, :], std[:, :]))
                    for k in range(TT):
                        last = nc.vector.tensor_scalar(Y[:, k, :], Z[:, k, :], mv[:, k, 0:1], rstd[:, k:k + 1],
                                                       ALU.subtract, ALU.mult)
                    last.then_inc(s["y_ready"], 1)
                    assert own[0] == STEPS

        @block.tensor
        def _(pe):
            pe.wait_ge(s["rows_ready"], 1)
            pe.wait_ge(s["consts_set"], 4)
            nc.tensor.matmul(b_x[:, 0, 0:1], ones[0:ROWS, :], wide1[:, :], start=True, stop=True).then_inc(s["wide_summed"], 1)
            idf, idb = ident[0:ROWS, 0:ROWS], ident_b[0:ROWS, 0:ROWS]
            pe.wait_ge(s["rows_ready"], 3)
            pe.wait_ge(s["wide_ready"], 1)
            for g in range(GPR):
                if g:
                    pe.wait_ge(s["cols_taken"], g)
                for j in range(TPG):
                    e = slice((g * TPG + j) * P, (g * TPG + j + 1) * P)
                    nc.tensor.matmul(cols_ps[0][:, j, 0:ROWS], src_hi[:, e], idb, start=True, stop=False)
                    nc.tensor.matmul(cols_ps[0][:, j, 0:ROWS], src_lo[:, e], idb, start=False, stop=True)
                    nc.tensor.matmul(cols_ps[1][:, j, 0:ROWS], src_hi[:, e], idb, start=True, stop=True)
                    nc.tensor.matmul(cols_ps[2][:, j, 0:ROWS], src_lo[:, e], idb, start=True, stop=True)
                    nc.tensor.matmul(cols_ps[3][:, j, 0:ROWS], dst_rel[:, e], idf, start=True, stop=True)
                    last = nc.tensor.matmul(cols_ps[4][:, j, 0:ROWS], dst_f[:, e], idf, start=True, stop=True)
                last.then_inc(s["cols_made"], 1)
            pe.wait_ge(s["cols_taken"], GPR)
            pe.wait_ge(s["weights_loaded"], 96)
            nc.tensor.transpose(b_x[:, 0, :], w_lin_sb[:, :], ident[:, :])
            nc.tensor.transpose(b_x[:, 1, :], w_msg_sb[:, :], ident[:, :]).then_inc(s["wT_made"], 1)
            pe.wait_ge(s["wT_taken"], 1)
            pe.wait_ge(s["rows_ready"], 4)
            nc.tensor.matmul(b_x[:, 0, :], w_linT[:, :], wu_sb[:, 0, :], start=True, stop=True)
            nc.tensor.matmul(b_x[:, 1, :], w_msgT[:, :], wu_sb[:, 1, :], start=True, stop=True)
            nc.tensor.matmul(b_x[:, 2, :], b_msg_w[:, :], wu_sb[:, 1, :], start=True, stop=True)
            nc.tensor.matmul(b_x[0:1, 3, :], b_lin_c[:, :], wu_sb[:, 0, :], start=True, stop=False)
            nc.tensor.matmul(b_x[0:1, 3, :], ones[0:1, 0:1], b_upd_r[:, :], start=False, stop=True).then_inc(s["w_made"], 1)
            pe.wait_ge(s["w_taken"], 1)
            pe.wait_ge(s["x_loaded"], 32)
            nc.tensor.matmul(hist, zeros_b[:, :], zeros_b[:, 0:NT], start=True, stop=False)
            is_wide = nc.tensor.value_load(wide_i[0:1, 0:1], min_val=0, max_val=1)
            pe.sem_inc(s["rows_made"], WS)

            def spread(r, g):
                one = ident_b[0:ROWS, bass.ds(r, 1)].to_broadcast([ROWS, P])
                e = slice(g * GE, (g + 1) * GE)
                o = b_src[g % 2][:, :, :].rearrange("p j e -> p (j e)")
                nc.tensor.matmul(o, one, src_hi[:, e], start=True, stop=False)
                nc.tensor.matmul(o, one, src_lo[:, e], start=False, stop=True).then_inc(s["src_spread"], 1)

            def edge_loop(gathered):
                with pe.Fori(0, ROWS) as r:
                    for g in range(GPR):
                        i = r * GPR + g
                        b = g % 2
                        pe.wait_ge(s["before_ready"], i + 1)
                        pe.wait_ge(s["dup_taken"], i + 1)
                        for j in range(TPG):
                            last = nc.tensor.matmul(b_dup[:, j:j + 1], eq_before[:, b, j, :], one_b[:, :], start=True, stop=True)
                        last.then_inc(s["dup_made"], 1)
                        pe.wait_ge(s["key_hot"], i + 1)
                        for j in range(TPG):
                            last = nc.tensor.matmul(b_M[:, j, :], hot_key[:, b, j, :], eq[:, b, j, :], start=True, stop=True)
                        last.then_inc(s["M_made"], 1)
                        spread(r if g < GPR - 1 else r + 1, (g + 1) % GPR)
                        pe.wait_ge(s["hi_hot"], i + 1)
                        for j in range(TPG):
                            nc.tensor.matmul(hist, hot_lo[:, b, j, :], hot_hi[:, b, j, :], start=False, stop=False)
                        if gathered:
                            pe.wait_ge(win_gathered[g], (r + 1) * 16 * TPG)
                        else:
                            pe.wait_ge(win_loaded[g], (r + 1) * 16)
                        pe.wait_ge(s["M_taken"], i + 1)
                        pe.wait_ge(s["rows_taken"], i + 1)
                        for j in range(TPG):
                            last = nc.tensor.matmul(b_rows[:, j, :], M[:, b, j, :], win[:, g, j if gathered else 0, :], start=True, stop=True)
                        last.then_inc(s["rows_made"], 1)
                        if g == 1:
                            pe.wait_ge(s["x_copied"], r + 1)
                            nc.tensor.transpose(b_x[:, 0, :], x_now[:, :], ident[:, :]).then_inc(s["x_turned"], 1)
                        if g == 2:
                            pe.wait_ge(s["xT_taken"], r + 1)
                            nc.tensor.matmul(b_x[:, 1, :], xT[:, :], A[:, :], start=True, stop=False)
                            nc.tensor.matmul(b_x[:, 1, :], ones[0:1, :], const_row[:, :], start=False, stop=True).then_inc(s["base_made"], 1)

            spread(0, 0)
            with pe.If(is_wide == 0):
                edge_loop(False)
            with pe.Else():
                edge_loop(True)
            nc.tensor.matmul(hist, zeros_b[:, :], zeros_b[:, 0:NT], start=False, stop=True).then_inc(s["hist_final"], 1)
            with pe.Fori(0, TG // 2) as t:
                for b in range(2):
                    i = t * 2 + b

                    def turn(k):
                        nc.tensor.transpose(turned[(b + k) % 2], S[:, b, 0, k, :], ident[:, :]).then_inc(s["S_turned"], 1)
                    pe.wait_ge(s["S_summed"], i + 1)
                    turn(0)
                    for k in range(TT):
                        n = i * TT + k
                        if k + 1 < TT:
                            turn(k + 1)
                        pe.wait_ge(s["ST_taken"], n + 1)
                        pe.wait_ge(s["z_ready"], n + 1)
                        nc.tensor.matmul(h_ps[(b + k) % 2], ST[:, (b + k) % 2, :], B[:, :], start=True, stop=True).then_inc(s["h_made"], 1)


_INS = ["x", "src", "dst", "L0_gnn_W_lin", "L0_gnn_b_lin", "L0_gnn_W_msg", "L0_gnn_b_msg", "L0_gnn_W_upd", "L0_gnn_b_upd"]


def kernel(**inputs):
    import concourse.bacc as bacc
    from concourse.bass_utils import run_bass_kernel_spmd

    nc = bacc.Bacc("TRN2", target_bir_lowering=False, num_devices=1)
    arrays, args = {}, []
    for name in _INS:
        a = np.ascontiguousarray(inputs[name])
        arrays[f"in_{name}"] = a
        args.append(nc.dram_tensor(f"in_{name}", a.shape, mybir.dt.from_np(a.dtype), kind="ExternalInput").ap())
    shape = arrays["in_x"].shape
    out = nc.dram_tensor("out_0", shape, mybir.dt.float32, kind="ExternalOutput").ap()
    gnn_program(nc, *args, out)
    r = run_bass_kernel_spmd(nc, [arrays], core_ids=[0])
    return r.results[0]["out_0"]
```

```python
from contextlib import ExitStack

import numpy as np
import concourse.bass as bass
from concourse import mybir

P = 128


def gnn_program(nc, x, src, dst, w_lin, b_lin, w_msg, b_msg, w_upd, b_upd, out):
    f32, bf16, i32, u32 = mybir.dt.float32, mybir.dt.bfloat16, mybir.dt.int32, mybir.dt.uint32
    ALU, ACT, AX = mybir.AluOpType, mybir.ActivationFunctionType, mybir.AxisListType

    N, F = x.shape
    E = src.shape[0]
    TPG = 4
    GE = TPG * P
    GPR = 4
    RE = GPR * GE
    ROWS = -(-E // RE)
    FULL = E // RE
    REST = E - FULL * RE
    PADDED = FULL // 32 * 32
    PADK = REST // P
    G = ROWS * GPR
    CPR = GPR * TPG
    NT = -(-N // P)
    NFULL = N // P
    NREST = N - NFULL * P
    assert NT == ROWS and ROWS < P
    NACC = TPG
    AR = N + P
    HEAD = 2
    PLAN = [0, 0, 0, 1] + [0, 1] * 5 + [2, 0, 1] * 4 + [2] + [0, 1] + [0, 1, 2, 3]
    PLAN = PLAN[:HEAD * CPR - 4] + [0, 1, 2, 3]
    MORE = [PLAN.count(j) - HEAD * GPR for j in range(NACC)]
    ZERO_LOTS = 9, 3

    def landed(n):
        open_ = [max((m for m in range(n) if PLAN[m] == j), default=-1) for j in range(NACC) if j != PLAN[n]]
        return min([m for m in open_ if m >= 0] + [n])

    WS = GPR
    ZW = AR * F // P // 7
    assert ZW * 7 * P == AR * F
    TT = 7
    TG = NT // TT
    EPS = 1e-5

    acc = [nc.dram_tensor(f"sum{j}", [AR, F], f32, kind="Internal").ap() for j in range(NACC)]
    low_dram = nc.dram_tensor("window_low", [1, G], i32, kind="Internal").ap()

    ctx = ExitStack()
    with ctx:
        def sb(name, shape, dt):
            return ctx.enter_context(nc.sbuf_tensor(name, shape, dt))

        def ps(name, shape, dt=f32):
            return ctx.enter_context(nc.psum_tensor(name, shape, dt))

        def sem(name):
            return ctx.enter_context(nc.semaphore(name))

        x_sb = sb("x_sb", [P, NT, F], f32)
        base = sb("base", [P, NT, F], f32)
        flat = base[:, :, :].rearrange("p t f -> p (t f)")
        src_i = flat[0:ROWS, 0:RE].bitcast(i32)
        dst_i = flat[0:ROWS, RE:2 * RE].bitcast(i32)
        dst_f = flat[0:ROWS, 2 * RE:3 * RE]
        dst_rel = flat[0:ROWS, 3 * RE:4 * RE]
        src_hi_i = flat[0:ROWS, 4 * RE:5 * RE].bitcast(i32)
        src_lo_i = flat[0:ROWS, 5 * RE:6 * RE].bitcast(i32)
        src_hi = sb("src_hi", [ROWS, RE], bf16)
        src_lo = sb("src_lo", [ROWS, RE], bf16)
        S = sb("S", [P, 2, NACC, TT, F], f32)
        S_flat = S[:, :, :, :, :].rearrange("p b j k f -> p (b j k f)")

        def col_list(n, dt):
            a = S_flat[:, n * ROWS * CPR // 2:(n + (1 if dt == bf16 else 2)) * ROWS * CPR // 2]
            return (a if dt == f32 else a.bitcast(dt)).rearrange("p (r k) -> p r k", k=CPR)

        col_src = col_list(0, f32)
        col_key = col_list(2, f32)
        col_dst = col_list(4, u32)
        col_hi = col_list(6, bf16)
        col_lo = col_list(7, bf16)

        low_f = sb("low_f", [ROWS, GPR], f32)
        high_f = sb("high_f", [ROWS, GPR], f32)
        low_i = sb("low_i", [ROWS, GPR], i32)
        wide4 = sb("wide4", [ROWS, GPR], f32)
        wide1 = sb("wide1", [ROWS, 1], f32)
        narrow_rows = sb("narrow_rows", [ROWS, 1], f32)
        low_used = sb("low_used", [ROWS, GPR], f32)
        wide = sb("wide", [P, 1], f32)
        narrow = sb("narrow", [P, 1], f32)
        wide_edge = sb("wide_edge", [P, 1], f32)
        wide_i = sb("wide_i", [1, 1], i32)

        iota_i = sb("iota_i", [P, P], i32)
        iota_f = sb("iota_f", [P, P], f32)
        edge_f = sb("edge_f", [P, 1], f32)
        trash = sb("trash", [P, TPG], f32)
        ident = sb("ident", [P, P], f32)
        ident_b = sb("ident_b", [P, P], bf16)
        ones = sb("ones", [P, P], f32)
        zeros_b = sb("zeros_b", [P, P], bf16)
        one_b = sb("one_b", [P, 1], bf16)

        w_lin_sb = sb("w_lin_sb", [P, F], f32)
        w_msg_sb = sb("w_msg_sb", [P, F], f32)
        wu_sb = sb("wu_sb", [P, 2, F], f32)
        w_linT = sb("w_linT", [P, P], f32)
        w_msgT = sb("w_msgT", [P, P], f32)
        A = sb("A", [P, F], f32)
        B = sb("B", [P, F], f32)
        b_lin_c = sb("b_lin_c", [P, 1], f32)
        b_msg_c = sb("b_msg_c", [P, 1], f32)
        b_msg_w = sb("b_msg_w", [P, P], f32)
        b_upd_r = sb("b_upd_r", [1, F], f32)
        const_row = sb("const_row", [1, F], f32)
        bmsg_rep = sb("bmsg_rep", [P, F], f32)

        win = sb("win", [P, WS, TPG, F], f32)
        one_hots = sb("one_hots", [P, 4, 2, TPG, P], bf16)
        eq, eq_before, hot_key, hot_lo = [one_hots[:, n, :, :, :] for n in range(4)]
        hot_hi = sb("hot_hi", [P, 2, TPG, NT], bf16)
        M = sb("M", [P, 2, TPG, P], f32)
        rows = sb("rows", [P, GPR, TPG, F], f32)
        dup = sb("dup", [P, TPG], f32)
        idx = sb("idx", [P, GPR, TPG], u32)
        idx_x = sb("idx_x", [P, GPR, TPG], u32)
        zeros = sb("zeros", [P, ZW], f32)
        x_now = sb("x_now", [P, F], f32)
        xT = sb("xT", [P, P], f32)

        def over(a):
            return a[:, 0:2 * TT * F].rearrange("p (b k f) -> p b k f", b=2, k=TT)

        S_all = sb("S_all", [P, 2, TT, F], f32)
        S_01 = over(one_hots[:, :, :, :, :].rearrange("p n b j e -> p (n b j e)").bitcast(f32))
        inv = sb("inv", [P, NT], f32)
        some = sb("some", [P, NT], f32)
        cnt1 = sb("cnt1", [P, NT], f32)
        ST = M[:, 0, :, :]
        Z = over(win[:, :, :, :].rearrange("p a b f -> p (a b f)"))
        Y = over(rows[:, :, :, :].rearrange("p a b f -> p (a b f)"))
        O = over(zeros[:, :])
        stats = sb("stats", [P, TT, 6], f32)
        mv = sb("mv", [P, 2, TT, 2], f32)
        std = sb("std", [P, 2, TT], f32)
        eps = sb("eps", [P, 1], f32)
        rstd = sb("rstd", [P, 2, TT], f32)
        shift = sb("shift", [P, 2, TT], f32)

        b_src = [ps(f"b_src{i}", [P, TPG, P]) for i in range(2)]
        b_M = ps("b_M", [P, TPG, P])
        b_rows = ps("b_rows", [P, TPG, F])
        b_hist = ps("b_hist", [P, 512])
        b_const = ps("b_const", [P, 512])
        b_dup = ps("b_dup", [P, 512])
        b_x = ps("b_x", [P, 4, P])
        hist = b_hist[:, 0:NT]
        c_iota = b_const[:, 0:P]
        c_before = b_const[:, P:2 * P]
        c_iota_hi = b_const[:, 2 * P:2 * P + NT]
        cols_ps = [[b_src[0], b_src[1], b_M], [b_rows, b_hist[:, :].rearrange("p (j e) -> p j e", e=P),
                                               b_dup[:, :].rearrange("p (j e) -> p j e", e=P)]]

        names = ("edges_loaded x_loaded weights_loaded zeros_set low_stored pads_set src_pads iota_set "
                 "consts_set masked src_split src_turned src_taken key_turned key_taken dst_taken low_ready rows_ready wide_summed wide_ready wT_made wT_taken "
                 "w_made w_taken chain key_ready hist_zeroed "
                 "src_spread eq_ready before_ready key_hot lo_hot hi_hot M_made M_taken dup_made dup_taken "
                 "rows_made rows_taken idx_ready rows_free hist_made x_copied x_turned xT_taken base_made base_taken "
                 "pair_01 pair_23 S_summed S_turned ST_taken h_made z_ready y_ready gathering counts_ready Z_begun Z_half Z_ready normed inverted rstd_ready stats_ready aggregating mv_ready std_ready hist_final gather_idx").split()
        s = {n: sem("s_" + n) for n in names}
        win_loaded = [sem(f"s_win_loaded{i}") for i in range(WS)]
        win_gathered = [sem(f"s_win_gathered{i}") for i in range(WS)]
        zeroed = [sem(f"s_zeroed{j}") for j in range(2)]
        added = [sem(f"s_added{j}") for j in range(NACC)]
        S_loaded = [[sem(f"s_S{i}_loaded_{pair}") for pair in ("01", "23")] for i in range(2)]

        stored = [sem(f"s_stored{i}") for i in range(2)]
        turned = [b_src[i][:, 0, :] for i in range(2)]
        banks = [b_M, b_rows, b_x, b_dup[:, :].rearrange("p (j e) -> p j e", e=P)]
        h_ps = [[banks[2 * b + k // 4][:, k % 4, :] for k in range(TT)] for b in range(2)]

        def bc(a, n):
            return a.unsqueeze(2).to_broadcast([a.shape[0], a.shape[1], n])

        def by_row(a, g):
            return a[:, :, g * TPG:(g + 1) * TPG].rearrange("p r j -> p j r")

        def rep(a, n):
            return a.unsqueeze(1).to_broadcast([a.shape[0], n, a.shape[1]])

        block = ctx.enter_context(nc.Block())

        @block.sync
        def _(sp):
            for part, lst in ((dst_i, dst), (src_i, src)):
                sp.dma_start(part[0:PADDED, :], lst[0:PADDED * RE].rearrange("(r f) -> r f", f=RE)).then_inc(s["edges_loaded"], 16)
            sp.wait_ge(s["pads_set"], 2)
            sp.wait_ge(s["src_pads"], 1)
            for part, lst in ((dst_i, dst), (src_i, src)):
                sp.dma_start(part[PADDED:FULL, :], lst[PADDED * RE:FULL * RE].rearrange("(r f) -> r f", f=RE)).then_inc(s["edges_loaded"], 16)
                sp.dma_start(part[FULL:ROWS, 0:REST], lst[FULL * RE:E].rearrange("(r f) -> r f", r=1)).then_inc(s["edges_loaded"], 16)
            sp.wait_ge(s["zeros_set"], 1)

            def zero_part(n):
                if n >= 2:
                    sp.wait_ge(zeroed[n % 2], 16 * (n // 2))
                flat = acc[n // 7].rearrange("n f -> (n f)").rearrange("(a p w) -> a p w", a=7, w=ZW)
                sp.dma_start(flat[n % 7], zeros[:, :]).then_inc(zeroed[n % 2], 16)

            for n in range(7):
                zero_part(n)
            sp.wait_ge(s["low_stored"], 16)
            sp.wait_ge(s["wide_ready"], 1)
            is_wide = sp.value_load(wide_i[0:1, 0:1], min_val=0, max_val=1)
            sp.sem_inc(s["x_copied"], 1)

            def load_window(r, g):
                low = sp.value_load(low_dram[0:1, bass.ds(r * GPR + g, 1)], min_val=0, max_val=N - P)
                if not (isinstance(r, int) and r == 0):
                    sp.wait_ge(s["rows_made"], r * GPR + g + 1)
                sp.dma_start(win[:, g, 0, :], x[bass.ds(low, P), :]).then_inc(win_loaded[g], 16)

            def load_x(r):
                sp.wait_ge(s["x_copied"], r + 1)
                if isinstance(r, int) and r == NFULL:
                    sp.dma_start(x_sb[0:NREST, NFULL, :], x[NFULL * P:N, :]).then_inc(s["x_loaded"], 16)
                else:
                    sp.dma_start(x_sb[:, bass.ds(r, 1), :].rearrange("p a f -> p (a f)"), x[bass.ds(r * P, P), :]).then_inc(s["x_loaded"], 16)

            def load_rows(windows):
                parts = list(range(7, 7 * NACC))
                for r in range(HEAD):
                    for g in range(GPR):
                        if windows:
                            load_window(r, g)
                        if g == 0:
                            load_x(r)
                        if r or g == GPR - 1:
                            for n in parts[:ZERO_LOTS[0]] if not r else parts[:ZERO_LOTS[1]]:
                                zero_part(n)
                            parts = parts[ZERO_LOTS[0] if not r else ZERO_LOTS[1]:]
                assert not parts
                with sp.Fori(HEAD, ROWS - 1) as r:
                    for g in range(GPR):
                        if windows:
                            load_window(r, g)
                        if g == 0:
                            load_x(r)
                for g in range(GPR):
                    if windows:
                        load_window(ROWS - 1, g)
                    if g == 0:
                        load_x(ROWS - 1)

            with sp.If(is_wide == 0):
                load_rows(True)
            with sp.Else():
                load_rows(False)
            def load_sum(t, b, j):
                sp.dma_start(S[:, b, j, :, :], acc[j][bass.ds((t * 2 + b) * (TT * P), TT * P), :]
                             .rearrange("(t p) f -> p t f", p=P)).then_inc(S_loaded[b][j // 2], 16)

            for j in range(NACC):
                sp.wait_ge(added[j], 16 * (G + MORE[j]))
                load_sum(0, 0, j)
            for j in range(NACC):
                load_sum(0, 1, j)
            with sp.Fori(1, TG // 2) as t:
                for b in range(2):
                    for pair, read in enumerate((s["pair_01"], s["pair_23"])):
                        sp.wait_ge(read, t * 2 + b - 1)
                        load_sum(t, b, 2 * pair)
                        load_sum(t, b, 2 * pair + 1)

        @block.scalar
        def _(act):
            act.dma_start(w_lin_sb[:, :], w_lin).then_inc(s["weights_loaded"], 16)
            act.dma_start(w_msg_sb[:, :], w_msg).then_inc(s["weights_loaded"], 16)
            act.dma_start(wu_sb[:, :, :], w_upd.rearrange("(a p) f -> p a f", p=P)).then_inc(s["weights_loaded"], 16)
            act.dma_start(b_lin_c[:, :], b_lin.rearrange("(p a) -> p a", a=1)).then_inc(s["weights_loaded"], 16)
            act.dma_start(b_msg_c[:, :], b_msg.rearrange("(p a) -> p a", a=1)).then_inc(s["weights_loaded"], 16)
            act.dma_start(b_upd_r[:, :], b_upd.rearrange("(a f) -> a f", a=1)).then_inc(s["weights_loaded"], 16)
            act.wait_ge(s["masked"], 1)
            act.activation(src_hi[:, :], src_hi_i, ACT.Copy).then_inc(s["src_split"], 1)
            act.wait_ge(s["masked"], 2)
            act.activation(src_lo[:, :], src_lo_i, ACT.Copy).then_inc(s["src_split"], 1)
            act.wait_ge(s["low_ready"], 1)
            act.dma_start(low_dram.rearrange("a (r g) -> (a r) g", g=GPR), low_i[:, :]).then_inc(s["low_stored"], 16)
            for g in range(GPR):
                act.wait_ge(s["src_turned"], g + 1)
                for k, to in enumerate((col_hi, col_lo)):
                    act.activation(by_row(to, g), cols_ps[g % 2][k][:, :, 0:ROWS], ACT.Copy).then_inc(s["src_taken"], 1)
            act.wait_ge(s["key_taken"], GPR)
            act.activation(col_dst, col_key, ACT.Copy).then_inc(s["dst_taken"], 1)
            act.wait_ge(s["wT_made"], 1)
            act.activation(w_linT[:, :], b_x[:, 0, :], ACT.Copy)
            act.activation(w_msgT[:, :], b_x[:, 1, :], ACT.Copy).then_inc(s["wT_taken"], 1)
            act.wait_ge(s["w_made"], 1)
            act.activation(A[:, :], b_x[:, 0, :], ACT.Copy)
            act.activation(B[:, :], b_x[:, 1, :], ACT.Copy)
            act.activation(bmsg_rep[:, :], b_x[:, 2, :], ACT.Copy)
            act.activation(const_row[:, :], b_x[0:1, 3, :], ACT.Copy).then_inc(s["w_taken"], 1)
            act.sem_inc(s["rows_taken"], 1)
            with act.Fori(0, ROWS) as r:
                for g in range(GPR):
                    i = r * GPR + g
                    act.wait_ge(s["M_made"], i + 1)
                    act.activation(M[:, g % 2, :, :], b_M[:, :, :], ACT.Copy).then_inc(s["M_taken"], 1)
                    act.wait_ge(s["rows_made"], i + WS + 1)
                    act.wait_ge(s["rows_free"], TPG * (i + 1))
                    act.activation(rows[:, g, :, :], b_rows[:, :, :], ACT.Copy).then_inc(s["rows_taken"], 1)
                    if g == 0:
                        act.wait_ge(s["x_loaded"], 16 * (r + 1))
                        act.activation(x_now[:, :], x_sb[:, bass.ds(r, 1), :].rearrange("p a f -> p (a f)"), ACT.Copy).then_inc(s["x_copied"], 1)
                    if g == 1:
                        act.wait_ge(s["x_turned"], r + 1)
                        act.activation(xT[:, :], b_x[:, 0, :], ACT.Copy).then_inc(s["xT_taken"], 1)
                    if g == 2:
                        act.wait_ge(s["base_made"], r + 1)
                        act.activation(base[:, bass.ds(r, 1), :], b_x[:, 1:2, :], ACT.Copy).then_inc(s["base_taken"], 1)
            def copy_turned(i, b):
                for k in range(TT):
                    act.wait_ge(s["S_turned"], i * TT + k + 1)
                    act.activation(ST[:, (b + k) % 2, :], turned[(b + k) % 2], ACT.Copy).then_inc(s["ST_taken"], 1)

            def finish(t, b, first=False, last=False):
                i = t * 2 + b
                act.wait_ge(s["mv_ready"], i + 1)
                act.activation(std[:, b, :], mv[:, b, :, 1], ACT.Sqrt, bias=eps[:, :]).then_inc(s["std_ready"], 1)
                if not first:
                    act.wait_ge(stored[b], 16 * t)
                act.wait_ge(s["rstd_ready"], i + 1)
                for k in range(TT):
                    last_k = act.activation(O[:, b, k, :], Y[:, b, k, :], ACT.Identity, scale=rstd[:, b, k:k + 1],
                                            bias=shift[:, b, k:k + 1])
                last_k.then_inc(s["normed"], 1)
                act.wait_ge(s["normed"], i + 3)
                whole = TT - 1 if last else TT
                act.dma_start(out[bass.ds(i * (TT * P), whole * P), :].rearrange("(t p) f -> p t f", p=P),
                              O[:, b, 0:whole, :]).then_inc(stored[b], 16)
                if last:
                    act.dma_start(out[NFULL * P:N, :], O[0:NREST, b, whole, :]).then_inc(stored[b], 16)

            LAST = TG // 2 - 1
            act.sem_inc(s["normed"], 2)
            for b in range(2):
                copy_turned(b, b)
            for b in range(2):
                finish(0, b, first=True)
                copy_turned(b + 2, b)
            with act.Fori(1, LAST) as t:
                for b in range(2):
                    finish(t, b)
                    copy_turned(t * 2 + b + 2, b)
            finish(LAST, 0)
            finish(LAST, 1, last=True)
            act.wait_ge(stored[0], 16 * (LAST + 1))
            act.wait_ge(stored[1], 16 * (LAST + 2))

        @block.gpsimd
        def _(pool):
            pool.iota(src_i[PADDED:ROWS, PADK * P:RE].rearrange("r (k e) -> r k e", e=P), [[0, CPR - PADK], [1, P]], base=N, channel_multiplier=0).then_inc(s["src_pads"], 1)
            pool.wait_ge(s["src_pads"], 1)
            pool.iota(iota_i[:, :], [[1, P]], base=0, channel_multiplier=0).then_inc(s["iota_set"], 1)
            pool.memset(ident[:, :], 0.0).then_inc(s["consts_set"], 1)
            pool.memset(ones[:, :], 1.0).then_inc(s["consts_set"], 1)
            pool.wait_ge(s["consts_set"], 2)
            pool.affine_select(out=ident[:, :], in_=ident[:, :], compare_op=ALU.not_equal, fill=1.0, base=0,
                               pattern=[[-1, P]], channel_multiplier=1).then_inc(s["consts_set"], 1)
            pool.affine_select(out=xT[:, :], in_=ones[:, :], compare_op=ALU.is_gt, fill=0.0, base=0,
                               pattern=[[1, P]], channel_multiplier=-1).then_inc(s["consts_set"], 1)
            pool.wait_ge(s["wide_ready"], 1)
            is_wide = pool.value_load(wide_i[0:1, 0:1], min_val=0, max_val=1)
            pool.sem_inc(s["rows_free"], CPR)

            def add_rows(i, g):
                pool.wait_ge(s["rows_taken"], i + 2)
                pool.wait_ge(s["idx_ready"], i + 1)
                for j in range(TPG):
                    pool.wait_ge(added[j], 16 * (i + MORE[j]))
                    pool.sem_inc(s["rows_free"], 1)
                    pool.indirect_dma_start(out=acc[j], out_offset=bass.IndirectOffsetOnAxis(ap=idx[:, g, j:j + 1], axis=0),
                                            in_=rows[:, g, j, :], in_offset=None, compute_op=ALU.add).then_inc(added[j], 16)

            def add_first_rows(r, g):
                i = r * GPR + g
                pool.wait_ge(s["rows_taken"], i + 2)
                pool.wait_ge(s["idx_ready"], i + 1)
                for j in range(TPG):
                    n = i * TPG + j
                    to = PLAN[n]
                    if to not in PLAN[:n]:
                        for last in (7 * to + 5, 7 * to + 6):
                            pool.wait_ge(zeroed[last % 2], 16 * (last // 2 + 1))
                    else:
                        pool.wait_ge(added[to], 16 * PLAN[:n].count(to))
                        if landed(n) > landed(n - 1):
                            pool.sem_inc(s["rows_free"], landed(n) - landed(n - 1))
                    pool.indirect_dma_start(out=acc[to], out_offset=bass.IndirectOffsetOnAxis(ap=idx[:, g, j:j + 1], axis=0),
                                            in_=rows[:, g, j, :], in_offset=None, compute_op=ALU.add).then_inc(added[to], 16)

            def gather_rows(i, g):
                pool.wait_ge(s["rows_made"], i + 1)
                pool.wait_ge(s["gather_idx"], i + 1)
                pool.sem_inc(s["gathering"], 1)
                for j in range(TPG):
                    pool.indirect_dma_start(out=win[:, g, j, :], out_offset=None, in_=x,
                                            in_offset=bass.IndirectOffsetOnAxis(ap=idx_x[:, g, j:j + 1], axis=0)
                                            ).then_inc(win_gathered[g], 16)

            with pool.If(is_wide == 0):
                for r in range(HEAD):
                    for g in range(GPR):
                        add_first_rows(r, g)
                with pool.Fori(HEAD, ROWS) as r:
                    for g in range(GPR):
                        add_rows(r * GPR + g, g)
            with pool.Else():
                for r in range(HEAD):
                    for g in range(GPR):
                        gather_rows(r * GPR + g, g)
                        add_first_rows(r, g)
                with pool.Fori(HEAD, ROWS) as r:
                    for g in range(GPR):
                        gather_rows(r * GPR + g, g)
                        add_rows(r * GPR + g, g)

            def add_pair(t, b, first=False):
                if not first:
                    pool.wait_ge(s["S_summed"], t * 2 + b - 1)
                pool.wait_ge(S_loaded[b][0], (t + 1) * 32)
                pool.tensor_tensor(S_01[:, b, :, :], S[:, b, 0, :, :], S[:, b, 1, :, :], ALU.add).then_inc(s["pair_01"], 1)

            def make_Z(t, b):
                i = t * 2 + b
                tiles = bass.ds(i * TT, TT)
                pool.wait_ge(s["y_ready"], i + 1)
                pool.sem_inc(s["Z_begun"], 1)
                pool.tensor_tensor(Z[:, b, :, :], rep(bmsg_rep[:, :], TT), bc(some[:, tiles], F), ALU.mult).then_inc(s["Z_half"], 1)
                pool.wait_ge(s["Z_half"], i + 1)
                pool.sem_inc(s["Z_begun"], 1)
                pool.tensor_tensor(Z[:, b, :, :], Z[:, b, :, :], base[:, tiles, :], ALU.add).then_inc(s["Z_ready"], 1)

            pool.wait_ge(s["counts_ready"], 1)
            pool.wait_ge(s["base_taken"], ROWS)
            make_Z(0, 0)
            for b in range(2):
                add_pair(0, b, first=True)
            make_Z(0, 1)
            with pool.Fori(1, TG // 2) as t:
                for b in range(2):
                    add_pair(t, b)
                    make_Z(t, b)

        @block.vector
        def _(dve):
            links = [0]

            def link(ins):
                links[0] += 1
                ins.then_inc(s["chain"], 1)
                dve.wait_ge(s["chain"], links[0])

            nc.vector.memset(dst_i[PADDED:ROWS, REST:RE], N - 1).then_inc(s["pads_set"], 1)
            nc.vector.memset(zeros[:, :], 0.0).then_inc(s["zeros_set"], 1)
            nc.vector.memset(x_sb[:, NFULL, :], 0.0).then_inc(s["pads_set"], 1)
            nc.vector.memset(zeros_b[:, :], 0.0)
            nc.vector.memset(one_b[:, :], 1.0)
            nc.vector.memset(eps[:, :], EPS)
            dve.wait_ge(s["iota_set"], 1)
            link(nc.vector.tensor_copy(iota_f[:, :], iota_i[:, :]))
            link(nc.vector.tensor_copy(c_iota, iota_f[:, :]))
            link(nc.vector.tensor_scalar(c_iota_hi, iota_f[:, 0:NT], float(P), None, ALU.mult))
            dve.wait_ge(s["consts_set"], 4)
            link(nc.vector.tensor_copy(c_before, xT[:, :]))
            link(nc.vector.tensor_copy(ident_b[:, :], ident[:, :]))
            link(nc.vector.tensor_tensor(xT[:, :], ident[:, :], iota_f[:, :], ALU.mult))
            link(nc.vector.reduce_sum(edge_f[:, :], xT[:, :], AX.X))
            link(nc.vector.tensor_scalar(trash[:, :], edge_f[:, :].to_broadcast([P, TPG]), float(N), None, ALU.add))
            dve.wait_ge(s["edges_loaded"], 96)
            nc.vector.tensor_single_scalar(src_hi_i, src_i, 0x7FFFFF80, ALU.bitwise_and).then_inc(s["masked"], 1)
            nc.vector.tensor_single_scalar(src_lo_i, src_i, P - 1, ALU.bitwise_and).then_inc(s["masked"], 1)
            link(nc.vector.tensor_copy(dst_f, dst_i))
            d3 = dst_f.rearrange("r (g f) -> r g f", f=GE)
            link(nc.vector.tensor_reduce(low_f[:, :], d3, AX.X, ALU.min))
            link(nc.vector.tensor_scalar(low_f[:, :], low_f[:, :], float(N - P), None, ALU.min))
            nc.vector.tensor_copy(low_i[:, :], low_f[:, :]).then_inc(s["low_ready"], 1)
            link(nc.vector.tensor_reduce(high_f[:, :], d3, AX.X, ALU.max))
            link(nc.vector.tensor_tensor(high_f[:, :], high_f[:, :], low_f[:, :], ALU.subtract))
            link(nc.vector.tensor_scalar(wide4[:, :], high_f[:, :], P - 0.5, None, ALU.is_gt))
            nc.vector.reduce_max(wide1[:, :], wide4[:, :], AX.X).then_inc(s["rows_ready"], 1)
            dve.wait_ge(s["wide_summed"], 1)
            link(nc.vector.tensor_scalar(wide[:, :], b_x[:, 0, 0:1], 0.5, None, ALU.is_gt))
            nc.vector.tensor_copy(wide_i[:, :], wide[0:1, :]).then_inc(s["wide_ready"], 1)
            link(nc.vector.tensor_scalar(narrow[:, :], wide[:, :], -1.0, 1.0, ALU.mult, ALU.add))
            link(nc.vector.tensor_scalar(low_used[:, :], low_f[:, :], narrow[0:ROWS, :], None, ALU.mult))
            nc.vector.tensor_tensor(dst_rel.rearrange("r (g f) -> r g f", f=GE), d3, bc(low_used[:, :], GE),
                                    ALU.subtract).then_inc(s["rows_ready"], 1)
            link(nc.vector.tensor_tensor(wide_edge[:, :], wide[:, :], edge_f[:, :], ALU.mult))
            dve.wait_ge(s["src_taken"], 2 * GPR)
            link(nc.vector.tensor_tensor(col_src, col_hi, col_lo, ALU.add))
            for g in range(GPR):
                dve.wait_ge(s["key_turned"], g + 1)
                nc.vector.tensor_copy(by_row(col_key, g), cols_ps[g % 2][2][:, :, 0:ROWS]).then_inc(s["key_taken"], 1)
            dve.wait_ge(s["key_taken"], GPR)
            dve.wait_ge(s["dst_taken"], 1)
            nc.vector.tensor_scalar(col_key, col_key, narrow[:, :], wide_edge[:, :], ALU.mult,
                                    ALU.add).then_inc(s["key_ready"], 1)
            dve.wait_ge(s["key_ready"], 1)
            dve.wait_ge(s["weights_loaded"], 96)
            nc.vector.tensor_copy(b_msg_w[:, :], b_msg_c[:, :].to_broadcast([P, P])).then_inc(s["rows_ready"], 1)
            dve.sem_inc(s["dup_taken"], 1)

            with dve.Fori(0, ROWS) as r:
                for g in range(GPR):
                    i = r * GPR + g
                    cols = slice(g * TPG, (g + 1) * TPG)

                    def col(a):
                        return a[:, bass.ds(r, 1), cols].rearrange("p a k -> p (a k)")
                    b = g % 2
                    dve.wait_ge(s["src_spread"], i + 1)
                    nc.vector.tensor_tensor(eq[:, b, :, :], b_src[b][:, :, :], bc(col(col_src), P), ALU.is_equal).then_inc(s["eq_ready"], 1)
                    nc.vector.tensor_tensor(hot_key[:, b, :, :], rep(c_iota, TPG), bc(col(col_key), P), ALU.is_equal).then_inc(s["key_hot"], 1)
                    dve.wait_ge(s["eq_ready"], i + 1)
                    nc.vector.tensor_tensor(eq_before[:, b, :, :], rep(c_before, TPG), eq[:, b, :, :], ALU.mult).then_inc(s["before_ready"], 1)
                    dve.wait_ge(s["rows_free"], TPG * (i + 1))
                    nc.vector.tensor_copy(idx_x[:, g, :], col(col_dst)).then_inc(s["gather_idx"], 1)
                    nc.vector.tensor_tensor(hot_lo[:, b, :, :], rep(c_iota, TPG), bc(col(col_lo), P), ALU.is_equal).then_inc(s["lo_hot"], 1)
                    nc.vector.tensor_tensor(hot_hi[:, b, :, :], rep(c_iota_hi, TPG), bc(col(col_hi), NT), ALU.is_equal).then_inc(s["hi_hot"], 1)
                    dve.wait_ge(s["dup_made"], i + 1)
                    nc.vector.scalar_tensor_tensor(out=dup[:, :], in0=b_dup[:, 0:TPG], scalar=1.0, in1=trash[:, :],
                                                   op0=ALU.min, op1=ALU.mult).then_inc(s["dup_taken"], 1)
                    dve.wait_ge(s["dup_taken"], i + 2)
                    nc.vector.tensor_tensor(idx[:, g, :], dup[:, :], col(col_src), ALU.max).then_inc(s["idx_ready"], 1)

            dve.wait_ge(s["hist_final"], 1)
            link(nc.vector.tensor_scalar(some[:, :], hist, 1.0, None, ALU.min))
            link(nc.vector.tensor_scalar(cnt1[:, :], hist, 1.0, None, ALU.max))
            link(nc.vector.reciprocal(inv[:, :], cnt1[:, :]))
            dve.sem_inc(s["counts_ready"], 1)
            dve.sem_inc(s["y_ready"], 2)

            def add_up(t, b):
                i = t * 2 + b
                dve.wait_ge(S_loaded[b][1], (t + 1) * 32)
                nc.vector.tensor_tensor(S_all[:, b, :, :], S[:, b, 2, :, :], S[:, b, 3, :, :], ALU.add).then_inc(s["pair_23"], 1)
                dve.wait_ge(s["pair_23"], i + 1)
                dve.wait_ge(s["pair_01"], i + 1)
                nc.vector.tensor_tensor(S_all[:, b, :, :], S_01[:, b, :, :], S_all[:, b, :, :], ALU.add).then_inc(s["S_summed"], 1)

            def trip(t, b, last=False):
                i = t * 2 + b
                dve.wait_ge(s["Z_ready"], i + 1)
                dve.wait_ge(s["normed"], i + 1)
                for k in range(TT):
                    n = i * TT + k
                    if k % 4 == 0:
                        dve.wait_ge(s["h_made"], i * TT + min(k + 4, TT))
                    nc.vector.scalar_tensor_tensor(
                        out=Y[:, b, k, :], in0=h_ps[b][k], scalar=inv[:, bass.ds(n, 1)],
                        in1=Z[:, b, k, :], op0=ALU.mult, op1=ALU.add).then_inc(s["z_ready"], 1)
                dve.wait_ge(s["z_ready"], (i + 1) * TT)
                nc.vector.scalar_tensor_tensor(out=Y[:, b, :, :], in0=Y[:, b, :, :], scalar=0.0, in1=x_sb[:, bass.ds(i * TT, TT), :],
                                               op0=ALU.max, op1=ALU.add).then_inc(s["y_ready"], 1)
                dve.wait_ge(s["y_ready"], i + 3)
                for k in range(TT):
                    last_k = nc.vector.bn_stats(stats[:, k, :], Y[:, b, k, :])
                last_k.then_inc(s["stats_ready"], 1)
                dve.wait_ge(s["stats_ready"], i + 1)
                dve.sem_inc(s["aggregating"], 1)
                for k in range(TT):
                    last_k = nc.vector.bn_aggr(mv[:, b, k, :], stats[:, k, :])
                last_k.then_inc(s["mv_ready"], 1)
                if not last:
                    add_up(t + 1, b)
                dve.wait_ge(s["std_ready"], i + 1)
                nc.vector.reciprocal(rstd[:, b, :], std[:, b, :]).then_inc(s["inverted"], 1)
                dve.wait_ge(s["inverted"], i + 1)
                nc.vector.scalar_tensor_tensor(out=shift[:, b, :], in0=mv[:, b, :, 0], scalar=-1.0, in1=rstd[:, b, :],
                                               op0=ALU.mult, op1=ALU.mult).then_inc(s["rstd_ready"], 1)

            for b in range(2):
                add_up(0, b)
            with dve.Fori(0, TG // 2 - 1) as t:
                for b in range(2):
                    trip(t, b)
            for b in range(2):
                trip(TG // 2 - 1, b, last=True)

        @block.tensor
        def _(pe):
            idf, idb = ident[0:ROWS, 0:ROWS], ident_b[0:ROWS, 0:ROWS]
            pe.wait_ge(s["src_split"], 2)
            for g in range(GPR):
                if g >= 2:
                    pe.wait_ge(s["src_taken"], 2 * (g - 1))
                for j in range(TPG):
                    e = slice((g * TPG + j) * P, (g * TPG + j + 1) * P)
                    nc.tensor.matmul(cols_ps[g % 2][0][:, j, 0:ROWS], src_hi[:, e], idb, start=True, stop=True)
                    last = nc.tensor.matmul(cols_ps[g % 2][1][:, j, 0:ROWS], src_lo[:, e], idb, start=True, stop=True)
                last.then_inc(s["src_turned"], 1)
            pe.wait_ge(s["rows_ready"], 1)
            pe.wait_ge(s["consts_set"], 4)
            nc.tensor.matmul(b_x[:, 0, 0:1], ones[0:ROWS, :], wide1[:, :], start=True, stop=True).then_inc(s["wide_summed"], 1)
            pe.wait_ge(s["rows_ready"], 2)
            for g in range(GPR):
                if g >= 2:
                    pe.wait_ge(s["key_taken"], g - 1)
                for j in range(TPG):
                    e = slice((g * TPG + j) * P, (g * TPG + j + 1) * P)
                    last = nc.tensor.matmul(cols_ps[g % 2][2][:, j, 0:ROWS], dst_rel[:, e], idf, start=True, stop=True)
                last.then_inc(s["key_turned"], 1)
            pe.wait_ge(s["key_taken"], GPR)
            pe.wait_ge(s["weights_loaded"], 96)
            nc.tensor.transpose(b_x[:, 0, :], w_lin_sb[:, :], ident[:, :])
            nc.tensor.transpose(b_x[:, 1, :], w_msg_sb[:, :], ident[:, :]).then_inc(s["wT_made"], 1)
            pe.wait_ge(s["wT_taken"], 1)
            pe.wait_ge(s["rows_ready"], 3)
            nc.tensor.matmul(b_x[:, 0, :], w_linT[:, :], wu_sb[:, 0, :], start=True, stop=True)
            nc.tensor.matmul(b_x[:, 1, :], w_msgT[:, :], wu_sb[:, 1, :], start=True, stop=True)
            nc.tensor.matmul(b_x[:, 2, :], b_msg_w[:, :], wu_sb[:, 1, :], start=True, stop=True)
            nc.tensor.matmul(b_x[0:1, 3, :], b_lin_c[:, :], wu_sb[:, 0, :], start=True, stop=False)
            nc.tensor.matmul(b_x[0:1, 3, :], ones[0:1, 0:1], b_upd_r[:, :], start=False, stop=True).then_inc(s["w_made"], 1)
            pe.wait_ge(s["w_taken"], 1)
            nc.tensor.matmul(hist, zeros_b[:, :], zeros_b[:, 0:NT], start=True, stop=False)
            is_wide = nc.tensor.value_load(wide_i[0:1, 0:1], min_val=0, max_val=1)
            pe.sem_inc(s["rows_made"], WS)

            def spread(r, g):
                one = ident_b[0:ROWS, bass.ds(r, 1)].to_broadcast([ROWS, P])
                e = slice(g * GE, (g + 1) * GE)
                o = b_src[g % 2][:, :, :].rearrange("p j e -> p (j e)")
                nc.tensor.matmul(o, one, src_hi[:, e], start=True, stop=False)
                nc.tensor.matmul(o, one, src_lo[:, e], start=False, stop=True).then_inc(s["src_spread"], 1)

            def edge_loop(gathered):
                with pe.Fori(0, ROWS) as r:
                    for g in range(GPR):
                        i = r * GPR + g
                        b = g % 2
                        pe.wait_ge(s["before_ready"], i + 1)
                        pe.wait_ge(s["dup_taken"], i + 1)
                        for j in range(TPG):
                            last = nc.tensor.matmul(b_dup[:, j:j + 1], eq_before[:, b, j, :], one_b[:, :], start=True, stop=True)
                        last.then_inc(s["dup_made"], 1)
                        pe.wait_ge(s["key_hot"], i + 1)
                        for j in range(TPG):
                            last = nc.tensor.matmul(b_M[:, j, :], hot_key[:, b, j, :], eq[:, b, j, :], start=True, stop=True)
                        last.then_inc(s["M_made"], 1)
                        spread(r if g < GPR - 1 else r + 1, (g + 1) % GPR)
                        pe.wait_ge(s["hi_hot"], i + 1)
                        for j in range(TPG):
                            nc.tensor.matmul(hist, hot_lo[:, b, j, :], hot_hi[:, b, j, :], start=False, stop=False)
                        if gathered:
                            pe.wait_ge(win_gathered[g], (r + 1) * 16 * TPG)
                        else:
                            pe.wait_ge(win_loaded[g], (r + 1) * 16)
                        pe.wait_ge(s["M_taken"], i + 1)
                        pe.wait_ge(s["rows_taken"], i + 1)
                        for j in range(TPG):
                            last = nc.tensor.matmul(b_rows[:, j, :], M[:, b, j, :], win[:, g, j if gathered else 0, :], start=True, stop=True)
                        last.then_inc(s["rows_made"], 1)
                        if g == 1:
                            pe.wait_ge(s["x_copied"], r + 2)
                            nc.tensor.transpose(b_x[:, 0, :], x_now[:, :], ident[:, :]).then_inc(s["x_turned"], 1)
                        if g == 2:
                            pe.wait_ge(s["xT_taken"], r + 1)
                            nc.tensor.matmul(b_x[:, 1, :], xT[:, :], A[:, :], start=True, stop=False)
                            nc.tensor.matmul(b_x[:, 1, :], ones[0:1, :], const_row[:, :], start=False, stop=True).then_inc(s["base_made"], 1)

            spread(0, 0)
            with pe.If(is_wide == 0):
                edge_loop(False)
            with pe.Else():
                edge_loop(True)
            nc.tensor.matmul(hist, zeros_b[:, :], zeros_b[:, 0:NT], start=False, stop=True).then_inc(s["hist_final"], 1)
            with pe.Fori(0, TG // 2) as t:
                for b in range(2):
                    i = t * 2 + b

                    def turn(k):
                        nc.tensor.transpose(turned[(b + k) % 2], S_all[:, b, k, :], ident[:, :]).then_inc(s["S_turned"], 1)
                    pe.wait_ge(s["S_summed"], i + 1)
                    pe.wait_ge(s["y_ready"], i + 1)
                    turn(0)
                    for k in range(TT):
                        n = i * TT + k
                        if k + 1 < TT:
                            turn(k + 1)
                        pe.wait_ge(s["ST_taken"], n + 1)
                        nc.tensor.matmul(h_ps[b][k], ST[:, (b + k) % 2, :], B[:, :], start=True, stop=True).then_inc(s["h_made"], 1)


_INS = ["x", "src", "dst", "L0_gnn_W_lin", "L0_gnn_b_lin", "L0_gnn_W_msg", "L0_gnn_b_msg", "L0_gnn_W_upd", "L0_gnn_b_upd"]


def kernel(**inputs):
    import concourse.bacc as bacc
    from concourse.bass_utils import run_bass_kernel_spmd

    nc = bacc.Bacc("TRN2", target_bir_lowering=False, num_devices=1)
    arrays, args = {}, []
    for name in _INS:
        a = np.ascontiguousarray(inputs[name])
        arrays[f"in_{name}"] = a
        args.append(nc.dram_tensor(f"in_{name}", a.shape, mybir.dt.from_np(a.dtype), kind="ExternalInput").ap())
    shape = arrays["in_x"].shape
    out = nc.dram_tensor("out_0", shape, mybir.dt.float32, kind="ExternalOutput").ap()
    gnn_program(nc, *args, out)
    r = run_bass_kernel_spmd(nc, [arrays], core_ids=[0])
    return r.results[0]["out_0"]
```

```python
from contextlib import ExitStack

import numpy as np
import concourse.bass as bass
from concourse import mybir

P = 128


def gnn_program(nc, x, src, dst, w_lin, b_lin, w_msg, b_msg, w_upd, b_upd, out):
    f32, bf16, i32, u32 = mybir.dt.float32, mybir.dt.bfloat16, mybir.dt.int32, mybir.dt.uint32
    ALU, ACT, AX = mybir.AluOpType, mybir.ActivationFunctionType, mybir.AxisListType

    N, F = x.shape
    E = src.shape[0]
    TPG = 4
    GE = TPG * P
    GPR = 4
    RE = GPR * GE
    ROWS = -(-E // RE)
    FULL = E // RE
    REST = E - FULL * RE
    PADDED = FULL // 32 * 32
    PADK = REST // P
    G = ROWS * GPR
    CPR = GPR * TPG
    REAL = -(-E // P) - (ROWS - 1) * CPR
    NT = -(-N // P)
    NFULL = N // P
    NREST = N - NFULL * P
    assert NT == ROWS and ROWS < P
    NACC = TPG
    AR = N + P
    HEAD = 2
    PLAN = [0, 0] + [0, 1] * 5 + [2, 0, 1] * 9
    PLAN = PLAN[:HEAD * CPR - 4] + [0, 1, 2, 3]
    MORE = [PLAN.count(j) - HEAD * GPR for j in range(NACC)]
    ZERO_LOTS = (2, 2, 2, 6), (8, 8, 7, 7)

    ADDS = [(ROWS - 1) * GPR + MORE[j] + len(range(j, REAL, TPG)) for j in range(NACC)]

    def landed(n):
        open_ = [max((m for m in range(n) if PLAN[m] == j), default=-1) for j in range(NACC) if j != PLAN[n]]
        return min([m for m in open_ if m >= 0] + [n])

    MORE_HIST = 2
    EARLY = -(-G // (GPR + MORE_HIST))
    AHEAD = (G - EARLY * GPR) // MORE_HIST
    assert EARLY * GPR + AHEAD * MORE_HIST == G
    PHASES = (0, AHEAD), (AHEAD, EARLY), (EARLY, ROWS)
    TPR = 3
    assert TPR * (ROWS - EARLY) <= ROWS - 1
    WS = GPR
    PARTS = 14
    ZERO_LAG = 3
    ZW = AR * F // P // PARTS
    assert ZW * PARTS * P == AR * F
    TT = 7
    TG = NT // TT
    EPS = 1e-5

    acc = [nc.dram_tensor(f"sum{j}", [AR, F], f32, kind="Internal").ap() for j in range(NACC)]
    low_dram = nc.dram_tensor("window_low", [1, G], i32, kind="Internal").ap()

    ctx = ExitStack()
    with ctx:
        def sb(name, shape, dt):
            return ctx.enter_context(nc.sbuf_tensor(name, shape, dt))

        def ps(name, shape, dt=f32):
            return ctx.enter_context(nc.psum_tensor(name, shape, dt))

        def sem(name):
            return ctx.enter_context(nc.semaphore(name))

        x_sb = sb("x_sb", [P, NT, F], f32)
        base = sb("base", [P, NT, F], f32)
        flat = base[:, :, :].rearrange("p t f -> p (t f)")
        src_i = flat[0:ROWS, 0:RE].bitcast(i32)
        dst_i = flat[0:ROWS, RE:2 * RE].bitcast(i32)
        dst_f = flat[0:ROWS, 2 * RE:3 * RE]
        low_diag = flat[0:ROWS, 3 * RE:3 * RE + GPR * ROWS].rearrange("r (g c) -> r g c", g=GPR)
        src_hi_i = flat[0:ROWS, 4 * RE:5 * RE].bitcast(i32)
        src_lo_i = flat[0:ROWS, 5 * RE:6 * RE].bitcast(i32)
        src_hi = sb("src_hi", [ROWS, RE], bf16)
        src_lo = sb("src_lo", [ROWS, RE], bf16)
        S = sb("S", [P, 2, NACC, TT, F], f32)
        S_flat = S[:, :, :, :, :].rearrange("p b j k f -> p (b j k f)")

        def col_list(n, dt):
            a = S_flat[:, n * ROWS * CPR // 2:(n + (1 if dt == bf16 else 2)) * ROWS * CPR // 2]
            return (a if dt == f32 else a.bitcast(dt)).rearrange("p (r k) -> p r k", k=CPR)

        col_src = col_list(0, f32)
        col_key = col_list(2, f32)
        col_dst = col_list(4, u32)
        col_hi = col_list(6, bf16)
        col_lo = col_list(7, bf16)

        low_f = sb("low_f", [ROWS, GPR], f32)
        high_f = sb("high_f", [ROWS, GPR], f32)
        low_i = sb("low_i", [ROWS, GPR], i32)
        wide4 = sb("wide4", [ROWS, GPR], f32)
        wide1 = sb("wide1", [ROWS, 1], f32)
        wide = sb("wide", [P, 1], f32)
        narrow = sb("narrow", [P, 1], f32)
        wide_edge = sb("wide_edge", [P, 1], f32)
        wide_i = sb("wide_i", [1, 1], i32)

        iota_i = sb("iota_i", [P, P], i32)
        iota_f = sb("iota_f", [P, P], f32)
        edge_f = sb("edge_f", [P, 1], f32)
        trash = sb("trash", [P, TPG], f32)
        ident = sb("ident", [P, P], f32)
        ident_b = sb("ident_b", [P, P], bf16)
        ones = sb("ones", [P, P], f32)
        zeros_b = sb("zeros_b", [P, P], bf16)
        one_b = sb("one_b", [P, 1], bf16)

        w_lin_sb = sb("w_lin_sb", [P, F], f32)
        w_msg_sb = sb("w_msg_sb", [P, F], f32)
        wu_sb = sb("wu_sb", [P, 2, F], f32)
        w_linT = sb("w_linT", [P, P], f32)
        w_msgT = sb("w_msgT", [P, P], f32)
        A = sb("A", [P, F], f32)
        B = sb("B", [P, F], f32)
        b_lin_c = sb("b_lin_c", [P, 1], f32)
        b_msg_c = sb("b_msg_c", [P, 1], f32)
        b_msg_w = sb("b_msg_w", [P, P], f32)
        b_upd_r = sb("b_upd_r", [1, F], f32)
        const_row = sb("const_row", [1, F], f32)
        bmsg_rep = sb("bmsg_rep", [P, F], f32)

        win = sb("win", [P, WS, TPG, F], f32)
        one_hots = sb("one_hots", [P, 4, 2, TPG, P], bf16)
        eq, eq_before, hot_key, hot_lo = [one_hots[:, n, :, :, :] for n in range(4)]
        hot_hi = sb("hot_hi", [P, 3, TPG, NT], bf16)
        spare = S_flat[:, 4 * ROWS * CPR:].bitcast(bf16)
        more_lo = [spare[:, n * GE:(n + 1) * GE].rearrange("p (j e) -> p j e", e=P) for n in range(2)]
        more_hi = [hot_hi[:, 2, :, :], spare[:, 2 * GE:2 * GE + TPG * NT].rearrange("p (j t) -> p j t", t=NT)]
        M = sb("M", [P, 2, TPG, P], f32)
        rows = sb("rows", [P, GPR, TPG, F], f32)
        dup = sb("dup", [P, TPG], f32)
        idx = sb("idx", [P, GPR, TPG], u32)
        idx_x = sb("idx_x", [P, GPR, TPG], u32)
        zeros = sb("zeros", [P, max(ZW, 2 * TT * F)], f32)
        x_now = sb("x_now", [P, F], f32)
        xT = sb("xT", [P, P], f32)

        def over(a):
            return a[:, 0:2 * TT * F].rearrange("p (b k f) -> p b k f", b=2, k=TT)

        S_all = sb("S_all", [P, 2, TT, F], f32)
        S_23 = over(one_hots[:, :, :, :, :].rearrange("p n b j e -> p (n b j e)").bitcast(f32))
        low_cols = S_all[:, :, :, :].rearrange("p b k f -> p (b k f)")[:, 0:GPR * ROWS]
        inv = sb("inv", [P, NT], f32)
        some = sb("some", [P, NT], f32)
        cnt1 = sb("cnt1", [P, NT], f32)
        ST = M[:, :, :, :].rearrange("p b j e -> p (b j) e")
        Y = over(rows[:, :, :, :].rearrange("p a b f -> p (a b f)"))
        O = over(zeros[:, :])
        stats = sb("stats", [P, TT, 6], f32)
        mv = sb("mv", [P, 2, TT, 2], f32)
        std = sb("std", [P, 2, TT], f32)
        eps = sb("eps", [P, 1], f32)
        rstd = sb("rstd", [P, 2, TT], f32)
        shift = sb("shift", [P, 2, TT], f32)

        b_src = [ps(f"b_src{i}", [P, TPG, P]) for i in range(2)]
        b_M = ps("b_M", [P, TPG, P])
        b_rows = ps("b_rows", [P, TPG, F])
        b_hist = ps("b_hist", [P, 512])
        b_const = ps("b_const", [P, 512])
        b_dup = ps("b_dup", [P, 512])
        b_x = ps("b_x", [P, 4, P])
        b_x_flat = b_x[:, :, :].rearrange("p a f -> p (a f)")
        hist = b_hist[:, 0:NT]
        c_iota = b_const[:, 0:P]
        c_before = b_const[:, P:2 * P]
        c_iota_hi = b_const[:, 2 * P:2 * P + NT]
        cols_ps = [[b_src[0], b_src[1], b_M], [b_rows, b_hist[:, :].rearrange("p (j e) -> p j e", e=P),
                                               b_dup[:, :].rearrange("p (j e) -> p j e", e=P)]]

        names = ("edges_loaded x_loaded weights_loaded zeros_set low_stored pads_set src_pads iota_set "
                 "consts_set masked src_split src_turned src_taken dst_ready dst_turned dst_taken low_spread low_turned key_taken low_ready rows_ready wide_summed wide_ready wT_made wT_taken "
                 "w_made w_taken chain key_ready "
                 "src_spread eq_ready before_ready key_hot hi_hot M_made M_taken dup_made dup_taken "
                 "rows_made rows_taken idx_ready rows_free x_copied x_turned xT_taken base_made base_taken "
                 "pair_01 pair_23 S_summed S_turned ST_taken h_made z_ready y_ready gathering constant_added more_hi_hot normed inverted rstd_ready stats_ready aggregating mv_ready std_ready hist_final gather_idx").split()
        s = {n: sem("s_" + n) for n in names}
        win_loaded = [sem(f"s_win_loaded{i}") for i in range(WS)]
        win_gathered = [sem(f"s_win_gathered{i}") for i in range(WS)]
        zeroed = [sem(f"s_zeroed{j}") for j in range(ZERO_LAG)]
        added = [sem(f"s_added{j}") for j in range(NACC)]
        S_loaded = [[sem(f"s_S{i}_loaded_{pair}") for pair in ("01", "23")] for i in range(2)]

        stored = [sem(f"s_stored{i}") for i in range(2)]
        BANKS = [range(0, 4), range(4, TT)]
        banks = [b_M, b_rows, b_x, b_dup[:, :].rearrange("p (j e) -> p j e", e=P)]
        h_ps = [[banks[2 * b + k // 4][:, k % 4, :] for k in range(TT)] for b in range(2)]

        def bc(a, n):
            return a.unsqueeze(2).to_broadcast([a.shape[0], a.shape[1], n])

        def by_row(a, g):
            return a[:, :, g * TPG:(g + 1) * TPG].rearrange("p r j -> p j r")

        def rep(a, n):
            return a.unsqueeze(1).to_broadcast([a.shape[0], n, a.shape[1]])

        block = ctx.enter_context(nc.Block())

        @block.sync
        def _(sp):
            for part, lst in ((dst_i, dst), (src_i, src)):
                sp.dma_start(part[0:PADDED, :], lst[0:PADDED * RE].rearrange("(r f) -> r f", f=RE)).then_inc(s["edges_loaded"], 16)
            sp.wait_ge(s["pads_set"], 2)
            sp.wait_ge(s["src_pads"], 1)
            for part, lst in ((dst_i, dst), (src_i, src)):
                sp.dma_start(part[PADDED:FULL, :], lst[PADDED * RE:FULL * RE].rearrange("(r f) -> r f", f=RE)).then_inc(s["edges_loaded"], 16)
                sp.dma_start(part[FULL:ROWS, 0:REST], lst[FULL * RE:E].rearrange("(r f) -> r f", r=1)).then_inc(s["edges_loaded"], 16)
            sp.wait_ge(s["zeros_set"], 1)

            def zero_part(n):
                if n >= ZERO_LAG:
                    sp.wait_ge(zeroed[n % ZERO_LAG], 16 * (n // ZERO_LAG))
                flat = acc[n // PARTS].rearrange("n f -> (n f)").rearrange("(a p w) -> a p w", a=PARTS, w=ZW)
                sp.dma_start(flat[n % PARTS], zeros[:, 0:ZW]).then_inc(zeroed[n % ZERO_LAG], 16)

            for n in range(PARTS):
                zero_part(n)
            sp.wait_ge(s["low_stored"], 16)
            sp.wait_ge(s["wide_ready"], 1)
            is_wide = sp.value_load(wide_i[0:1, 0:1], min_val=0, max_val=1)
            sp.sem_inc(s["x_copied"], 1)

            def load_window(r, g):
                low = sp.value_load(low_dram[0:1, bass.ds(r * GPR + g, 1)], min_val=0, max_val=N - P)
                if not (isinstance(r, int) and r == 0):
                    sp.wait_ge(s["rows_made"], r * GPR + g + 1)
                sp.dma_start(win[:, g, 0, :], x[bass.ds(low, P), :]).then_inc(win_loaded[g], 16)

            def load_x(r):
                sp.wait_ge(s["x_copied"], r + 1)
                if isinstance(r, int) and r == NFULL:
                    sp.dma_start(x_sb[0:NREST, NFULL, :], x[NFULL * P:N, :]).then_inc(s["x_loaded"], 16)
                else:
                    sp.dma_start(x_sb[:, bass.ds(r, 1), :].rearrange("p a f -> p (a f)"), x[bass.ds(r * P, P), :]).then_inc(s["x_loaded"], 16)

            def load_rows(windows):
                parts = list(range(PARTS, PARTS * NACC))
                for r in range(HEAD):
                    for g in range(GPR):
                        if windows:
                            load_window(r, g)
                        if g == 0:
                            load_x(r)
                        for _ in range(ZERO_LOTS[r][g]):
                            zero_part(parts.pop(0))
                assert not parts
                with sp.Fori(HEAD, ROWS - 1) as r:
                    for g in range(GPR):
                        if windows:
                            load_window(r, g)
                        if g == 0:
                            load_x(r)
                for g in range(GPR):
                    if windows:
                        load_window(ROWS - 1, g)
                    if g == 0:
                        load_x(ROWS - 1)

            with sp.If(is_wide == 0):
                load_rows(True)
            with sp.Else():
                load_rows(False)
            def load_sum(t, b, j):
                sp.dma_start(S[:, b, j, :, :], acc[j][bass.ds((t * 2 + b) * (TT * P), TT * P), :]
                             .rearrange("(t p) f -> p t f", p=P)).then_inc(S_loaded[b][j // 2], 16)

            sp.wait_ge(s["idx_ready"], G)
            for j in range(NACC):
                sp.wait_ge(added[j], 16 * ADDS[j])
                load_sum(0, 0, j)
            for j in range(NACC):
                load_sum(0, 1, j)
            with sp.Fori(1, TG // 2) as t:
                for b in range(2):
                    for pair, read in enumerate((s["pair_01"], s["pair_23"])):
                        sp.wait_ge(read, t * 2 + b - 1)
                        load_sum(t, b, 2 * pair)
                        load_sum(t, b, 2 * pair + 1)

        @block.scalar
        def _(act):
            act.dma_start(w_lin_sb[:, :], w_lin).then_inc(s["weights_loaded"], 16)
            act.dma_start(w_msg_sb[:, :], w_msg).then_inc(s["weights_loaded"], 16)
            act.dma_start(wu_sb[:, :, :], w_upd.rearrange("(a p) f -> p a f", p=P)).then_inc(s["weights_loaded"], 16)
            act.dma_start(b_lin_c[:, :], b_lin.rearrange("(p a) -> p a", a=1)).then_inc(s["weights_loaded"], 16)
            act.dma_start(b_msg_c[:, :], b_msg.rearrange("(p a) -> p a", a=1)).then_inc(s["weights_loaded"], 16)
            act.dma_start(b_upd_r[:, :], b_upd.rearrange("(a f) -> a f", a=1)).then_inc(s["weights_loaded"], 16)
            act.wait_ge(s["masked"], 1)
            act.activation(src_hi[:, :], src_hi_i, ACT.Copy).then_inc(s["src_split"], 1)
            act.wait_ge(s["masked"], 2)
            act.activation(src_lo[:, :], src_lo_i, ACT.Copy).then_inc(s["src_split"], 1)
            act.wait_ge(s["low_ready"], 1)
            act.dma_start(low_dram.rearrange("a (r g) -> (a r) g", g=GPR), low_i[:, :]).then_inc(s["low_stored"], 16)
            for g in range(GPR):
                act.wait_ge(s["src_turned"], g + 1)
                for k, to in enumerate((col_hi, col_lo)):
                    act.activation(by_row(to, g), cols_ps[g % 2][k][:, :, 0:ROWS], ACT.Copy).then_inc(s["src_taken"], 1)
                act.wait_ge(s["dst_turned"], g + 1)
                act.activation(by_row(col_dst, g), cols_ps[g % 2][2][:, :, 0:ROWS], ACT.Copy).then_inc(s["dst_taken"], 1)
            act.wait_ge(s["wT_made"], 1)
            act.activation(w_linT[:, :], b_x[:, 0, :], ACT.Copy)
            act.activation(w_msgT[:, :], b_x[:, 1, :], ACT.Copy).then_inc(s["wT_taken"], 1)
            act.wait_ge(s["w_made"], 1)
            act.activation(A[:, :], b_x[:, 0, :], ACT.Copy)
            act.activation(B[:, :], b_x[:, 1, :], ACT.Copy)
            act.activation(bmsg_rep[:, :], b_x[:, 2, :], ACT.Copy)
            act.activation(const_row[:, :], b_x[0:1, 3, :], ACT.Copy).then_inc(s["w_taken"], 1)
            act.sem_inc(s["rows_taken"], 1)
            with act.Fori(0, ROWS) as r:
                for g in range(GPR):
                    i = r * GPR + g
                    act.wait_ge(s["M_made"], i + 1)
                    act.activation(M[:, g % 2, :, :], b_M[:, :, :], ACT.Copy).then_inc(s["M_taken"], 1)
                    act.wait_ge(s["rows_made"], i + WS + 1)
                    act.wait_ge(s["rows_free"], TPG * (i + 1))
                    act.activation(rows[:, g, :, :], b_rows[:, :, :], ACT.Copy).then_inc(s["rows_taken"], 1)
                    if g == 0:
                        act.wait_ge(s["x_loaded"], 16 * (r + 1))
                        act.activation(x_now[:, :], x_sb[:, bass.ds(r, 1), :].rearrange("p a f -> p (a f)"), ACT.Copy).then_inc(s["x_copied"], 1)
                    if g == 1:
                        act.wait_ge(s["x_turned"], r + 1)
                        act.activation(xT[:, :], b_x[:, 0, :], ACT.Copy).then_inc(s["xT_taken"], 1)
                    if g == 2:
                        act.wait_ge(s["base_made"], r + 1)
                        act.activation(base[:, bass.ds(r, 1), :], b_x[:, 1:2, :], ACT.Copy).then_inc(s["base_taken"], 1)
            def copy_turned(i):
                for q, tiles in enumerate(BANKS):
                    act.wait_ge(s["S_turned"], i * len(BANKS) + q + 1)
                    act.activation(ST[:, tiles.start:tiles.stop, :], b_src[q][:, 0:len(tiles), :], ACT.Copy).then_inc(s["ST_taken"], 1)

            def finish(t, b, first=False, final=False):
                i = t * 2 + b
                act.wait_ge(s["mv_ready"], i + 1)
                act.activation(std[:, b, :], mv[:, b, :, 1], ACT.Sqrt, bias=eps[:, :]).then_inc(s["std_ready"], 1)
                if not final:
                    copy_turned(i + 2)
                if not first:
                    act.wait_ge(stored[b], 16 * t)
                act.wait_ge(s["rstd_ready"], i + 1)
                for k in range(TT):
                    last_k = act.activation(O[:, b, k, :], Y[:, b, k, :], ACT.Identity, scale=rstd[:, b, k:k + 1],
                                            bias=shift[:, b, k:k + 1])
                last_k.then_inc(s["normed"], 1)
                act.wait_ge(s["normed"], i + 3)
                whole = TT - 1 if final and b == 1 else TT
                act.dma_start(out[bass.ds(i * (TT * P), whole * P), :].rearrange("(t p) f -> p t f", p=P),
                              O[:, b, 0:whole, :]).then_inc(stored[b], 16)
                if whole < TT:
                    act.dma_start(out[NFULL * P:N, :], O[0:NREST, b, whole, :]).then_inc(stored[b], 16)

            LAST = TG // 2 - 1
            act.sem_inc(s["normed"], 2)
            for b in range(2):
                copy_turned(b)
            for b in range(2):
                finish(0, b, first=True)
            with act.Fori(1, LAST) as t:
                for b in range(2):
                    finish(t, b)
            for b in range(2):
                finish(LAST, b, final=True)
            act.wait_ge(stored[0], 16 * (LAST + 1))
            act.wait_ge(stored[1], 16 * (LAST + 2))

        @block.gpsimd
        def _(pool):
            pool.iota(src_i[PADDED:ROWS, PADK * P:RE].rearrange("r (k e) -> r k e", e=P), [[0, CPR - PADK], [1, P]], base=N, channel_multiplier=0).then_inc(s["src_pads"], 1)
            pool.wait_ge(s["src_pads"], 1)
            pool.iota(iota_i[:, :], [[1, P]], base=0, channel_multiplier=0).then_inc(s["iota_set"], 1)
            pool.memset(ident[:, :], 0.0).then_inc(s["consts_set"], 1)
            pool.memset(ones[:, :], 1.0).then_inc(s["consts_set"], 1)
            pool.wait_ge(s["consts_set"], 2)
            pool.affine_select(out=ident[:, :], in_=ident[:, :], compare_op=ALU.not_equal, fill=1.0, base=0,
                               pattern=[[-1, P]], channel_multiplier=1).then_inc(s["consts_set"], 1)
            pool.affine_select(out=xT[:, :], in_=ones[:, :], compare_op=ALU.is_gt, fill=0.0, base=0,
                               pattern=[[1, P]], channel_multiplier=-1).then_inc(s["consts_set"], 1)
            pool.wait_ge(s["wide_ready"], 1)
            is_wide = pool.value_load(wide_i[0:1, 0:1], min_val=0, max_val=1)
            pool.sem_inc(s["rows_free"], CPR)

            def add_rows(i, g, tiles=TPG):
                pool.wait_ge(s["rows_taken"], i + 2)
                pool.wait_ge(s["idx_ready"], i + 1)
                for j in range(tiles):
                    pool.wait_ge(added[j], 16 * (i + MORE[j]))
                    pool.sem_inc(s["rows_free"], 1)
                    pool.indirect_dma_start(out=acc[j], out_offset=bass.IndirectOffsetOnAxis(ap=idx[:, g, j:j + 1], axis=0),
                                            in_=rows[:, g, j, :], in_offset=None, compute_op=ALU.add).then_inc(added[j], 16)

            def add_first_rows(r, g):
                i = r * GPR + g
                pool.wait_ge(s["rows_taken"], i + 2)
                pool.wait_ge(s["idx_ready"], i + 1)
                for j in range(TPG):
                    n = i * TPG + j
                    to = PLAN[n]
                    if to not in PLAN[:n]:
                        for last in range(PARTS * (to + 1) - ZERO_LAG, PARTS * (to + 1)):
                            pool.wait_ge(zeroed[last % ZERO_LAG], 16 * (last // ZERO_LAG + 1))
                    else:
                        pool.wait_ge(added[to], 16 * PLAN[:n].count(to))
                        if landed(n) > landed(n - 1):
                            pool.sem_inc(s["rows_free"], landed(n) - landed(n - 1))
                    pool.indirect_dma_start(out=acc[to], out_offset=bass.IndirectOffsetOnAxis(ap=idx[:, g, j:j + 1], axis=0),
                                            in_=rows[:, g, j, :], in_offset=None, compute_op=ALU.add).then_inc(added[to], 16)

            def gather_rows(i, g):
                pool.wait_ge(s["rows_made"], i + 1)
                pool.wait_ge(s["gather_idx"], i + 1)
                pool.sem_inc(s["gathering"], 1)
                for j in range(TPG):
                    pool.indirect_dma_start(out=win[:, g, j, :], out_offset=None, in_=x,
                                            in_offset=bass.IndirectOffsetOnAxis(ap=idx_x[:, g, j:j + 1], axis=0)
                                            ).then_inc(win_gathered[g], 16)

            with pool.If(is_wide == 0):
                for r in range(HEAD):
                    for g in range(GPR):
                        add_first_rows(r, g)
                with pool.Fori(HEAD, ROWS - 1) as r:
                    for g in range(GPR):
                        add_rows(r * GPR + g, g)
                for g in range(GPR):
                    add_rows((ROWS - 1) * GPR + g, g, min(TPG, max(REAL - g * TPG, 0)))
            with pool.Else():
                for r in range(HEAD):
                    for g in range(GPR):
                        gather_rows(r * GPR + g, g)
                        add_first_rows(r, g)
                with pool.Fori(HEAD, ROWS - 1) as r:
                    for g in range(GPR):
                        gather_rows(r * GPR + g, g)
                        add_rows(r * GPR + g, g)
                for g in range(GPR):
                    gather_rows((ROWS - 1) * GPR + g, g)
                    add_rows((ROWS - 1) * GPR + g, g, min(TPG, max(REAL - g * TPG, 0)))

            def add_up(t, b, first=False):
                i = t * 2 + b
                if not first:
                    pool.wait_ge(s["S_turned"], (i - 1) * len(BANKS))
                pool.wait_ge(S_loaded[b][0], (t + 1) * 32)
                pool.tensor_tensor(S_all[:, b, :, :], S[:, b, 0, :, :], S[:, b, 1, :, :], ALU.add).then_inc(s["pair_01"], 1)
                pool.wait_ge(s["pair_01"], i + 1)
                pool.wait_ge(s["pair_23"], i + 1)
                pool.tensor_tensor(S_all[:, b, :, :], S_all[:, b, :, :], S_23[:, b, :, :], ALU.add).then_inc(s["S_summed"], 1)

            for b in range(2):
                add_up(0, b, first=True)
            with pool.Fori(1, TG // 2) as t:
                for b in range(2):
                    add_up(t, b)

        @block.vector
        def _(dve):
            links = [0]

            def link(ins):
                links[0] += 1
                ins.then_inc(s["chain"], 1)
                dve.wait_ge(s["chain"], links[0])

            nc.vector.memset(dst_i[PADDED:ROWS, REST:RE], N - 1).then_inc(s["pads_set"], 1)
            nc.vector.memset(zeros[:, 0:ZW], 0.0).then_inc(s["zeros_set"], 1)
            nc.vector.memset(x_sb[:, NFULL, :], 0.0).then_inc(s["pads_set"], 1)
            nc.vector.memset(zeros_b[:, :], 0.0)
            nc.vector.memset(one_b[:, :], 1.0)
            nc.vector.memset(eps[:, :], EPS)
            dve.wait_ge(s["iota_set"], 1)
            link(nc.vector.tensor_copy(iota_f[:, :], iota_i[:, :]))
            link(nc.vector.tensor_copy(c_iota, iota_f[:, :]))
            link(nc.vector.tensor_scalar(c_iota_hi, iota_f[:, 0:NT], float(P), None, ALU.mult))
            dve.wait_ge(s["consts_set"], 4)
            link(nc.vector.tensor_copy(c_before, xT[:, :]))
            link(nc.vector.tensor_copy(ident_b[:, :], ident[:, :]))
            link(nc.vector.tensor_tensor(xT[:, :], ident[:, :], iota_f[:, :], ALU.mult))
            link(nc.vector.reduce_sum(edge_f[:, :], xT[:, :], AX.X))
            link(nc.vector.tensor_scalar(trash[:, :], edge_f[:, :].to_broadcast([P, TPG]), float(N), None, ALU.add))
            dve.wait_ge(s["edges_loaded"], 96)
            nc.vector.tensor_single_scalar(src_hi_i, src_i, 0x7FFFFF80, ALU.bitwise_and).then_inc(s["masked"], 1)
            nc.vector.tensor_single_scalar(src_lo_i, src_i, P - 1, ALU.bitwise_and).then_inc(s["masked"], 1)
            nc.vector.tensor_copy(dst_f, dst_i).then_inc(s["dst_ready"], 1)
            dve.wait_ge(s["dst_ready"], 1)
            d3 = dst_f.rearrange("r (g f) -> r g f", f=GE)
            link(nc.vector.tensor_reduce(low_f[:, :], d3, AX.X, ALU.min))
            link(nc.vector.tensor_scalar(low_f[:, :], low_f[:, :], float(N - P), None, ALU.min))
            nc.vector.tensor_copy(low_i[:, :], low_f[:, :]).then_inc(s["low_ready"], 1)
            nc.vector.tensor_tensor(low_diag, rep(ident[0:ROWS, 0:ROWS], GPR), bc(low_f[:, :], ROWS), ALU.mult).then_inc(s["low_spread"], 1)
            link(nc.vector.tensor_reduce(high_f[:, :], d3, AX.X, ALU.max))
            link(nc.vector.tensor_tensor(high_f[:, :], high_f[:, :], low_f[:, :], ALU.subtract))
            dve.wait_ge(s["low_turned"], 1)
            link(nc.vector.tensor_copy(low_cols, b_x_flat[:, 0:GPR * ROWS]))
            link(nc.vector.tensor_scalar(wide4[:, :], high_f[:, :], P - 0.5, None, ALU.is_gt))
            nc.vector.reduce_max(wide1[:, :], wide4[:, :], AX.X).then_inc(s["rows_ready"], 1)
            dve.wait_ge(s["wide_summed"], 1)
            link(nc.vector.tensor_scalar(wide[:, :], b_x[:, 0, 0:1], 0.5, None, ALU.is_gt))
            nc.vector.tensor_copy(wide_i[:, :], wide[0:1, :]).then_inc(s["wide_ready"], 1)
            link(nc.vector.tensor_scalar(narrow[:, :], wide[:, :], -1.0, 1.0, ALU.mult, ALU.add))
            link(nc.vector.tensor_tensor(wide_edge[:, :], wide[:, :], edge_f[:, :], ALU.mult))
            dve.wait_ge(s["weights_loaded"], 96)
            nc.vector.tensor_copy(b_msg_w[:, :], b_msg_c[:, :].to_broadcast([P, P])).then_inc(s["rows_ready"], 1)
            for g in range(GPR):
                dve.wait_ge(s["dst_taken"], g + 1)
                nc.vector.tensor_tensor(by_row(col_key, g), cols_ps[g % 2][2][:, :, 0:ROWS],
                                        rep(low_cols[:, g * ROWS:(g + 1) * ROWS], TPG), ALU.subtract).then_inc(s["key_taken"], 1)
            dve.wait_ge(s["src_taken"], 2 * GPR)
            link(nc.vector.tensor_tensor(col_src, col_hi, col_lo, ALU.add))
            dve.wait_ge(s["key_taken"], GPR)
            nc.vector.tensor_scalar(col_key, col_key, narrow[:, :], wide_edge[:, :], ALU.mult,
                                    ALU.add).then_inc(s["key_ready"], 1)
            dve.wait_ge(s["key_ready"], 1)
            dve.sem_inc(s["dup_taken"], 1)

            def flat_tiles(a):
                return a.rearrange("p r k -> p (r k)")

            def add_constant(n):
                dve.wait_ge(s["base_taken"], n + 1)
                here = base[:, bass.ds(n, 1), :].rearrange("p a f -> p (a f)")
                nc.vector.scalar_tensor_tensor(out=here, in0=bmsg_rep[:, :], scalar=some[:, bass.ds(n, 1)],
                                               in1=here, op0=ALU.mult, op1=ALU.add).then_inc(s["constant_added"], 1)

            def edge_row(r, phase):
                for g in range(GPR):
                    i = r * GPR + g
                    cols = slice(g * TPG, (g + 1) * TPG)

                    def col(a):
                        return a[:, bass.ds(r, 1), cols].rearrange("p a k -> p (a k)")
                    b = g % 2
                    dve.wait_ge(s["src_spread"], i + 1)
                    nc.vector.tensor_tensor(eq[:, b, :, :], b_src[b][:, :, :], bc(col(col_src), P), ALU.is_equal).then_inc(s["eq_ready"], 1)
                    nc.vector.tensor_tensor(hot_key[:, b, :, :], rep(c_iota, TPG), bc(col(col_key), P), ALU.is_equal).then_inc(s["key_hot"], 1)
                    dve.wait_ge(s["eq_ready"], i + 1)
                    nc.vector.tensor_tensor(eq_before[:, b, :, :], rep(c_before, TPG), eq[:, b, :, :], ALU.mult).then_inc(s["before_ready"], 1)
                    dve.wait_ge(s["rows_free"], TPG * (i + 1))
                    nc.vector.tensor_copy(idx_x[:, g, :], col(col_dst)).then_inc(s["gather_idx"], 1)
                    if phase < 2:
                        nc.vector.tensor_tensor(hot_lo[:, b, :, :], rep(c_iota, TPG), bc(col(col_lo), P), ALU.is_equal)
                        nc.vector.tensor_tensor(hot_hi[:, b, :, :], rep(c_iota_hi, TPG), bc(col(col_hi), NT), ALU.is_equal).then_inc(s["hi_hot"], 1)
                    if phase == 0 and g < MORE_HIST:
                        ahead = bass.ds((EARLY * GPR + r * MORE_HIST + g) * TPG, TPG)
                        nc.vector.tensor_tensor(more_lo[b], rep(c_iota, TPG), bc(flat_tiles(col_lo)[:, ahead], P), ALU.is_equal)
                        nc.vector.tensor_tensor(more_hi[b], rep(c_iota_hi, TPG), bc(flat_tiles(col_hi)[:, ahead], NT), ALU.is_equal).then_inc(s["more_hi_hot"], 1)
                    if phase == 2 and g == GPR - 1:
                        for k in range(TPR):
                            add_constant((r - EARLY) * TPR + k)
                    dve.wait_ge(s["dup_made"], i + 1)
                    nc.vector.scalar_tensor_tensor(out=dup[:, :], in0=b_dup[:, 0:TPG], scalar=1.0, in1=trash[:, :],
                                                   op0=ALU.min, op1=ALU.mult).then_inc(s["dup_taken"], 1)
                    dve.wait_ge(s["dup_taken"], i + 2)
                    nc.vector.tensor_tensor(idx[:, g, :], dup[:, :], col(col_src), ALU.max).then_inc(s["idx_ready"], 1)

            for phase in range(2):
                with dve.Fori(*PHASES[phase]) as r:
                    edge_row(r, phase)
            dve.wait_ge(s["hist_final"], 1)
            link(nc.vector.tensor_scalar(some[:, :], hist, 1.0, None, ALU.min))
            link(nc.vector.tensor_scalar(cnt1[:, :], hist, 1.0, None, ALU.max))
            link(nc.vector.reciprocal(inv[:, :], cnt1[:, :]))
            with dve.Fori(*PHASES[2]) as r:
                edge_row(r, 2)
            for n in range(TPR * (ROWS - EARLY), NT):
                add_constant(n)
            dve.sem_inc(s["y_ready"], 2)
            dve.wait_ge(s["constant_added"], NT)

            def add_pair(t, b, first=False):
                i = t * 2 + b
                if not first:
                    dve.wait_ge(s["S_summed"], i - 1)
                dve.wait_ge(S_loaded[b][1], (t + 1) * 32)
                nc.vector.tensor_tensor(S_23[:, b, :, :], S[:, b, 2, :, :], S[:, b, 3, :, :], ALU.add).then_inc(s["pair_23"], 1)

            def invert(t, b):
                dve.wait_ge(s["std_ready"], t * 2 + b + 1)
                nc.vector.reciprocal(rstd[:, b, :], std[:, b, :]).then_inc(s["inverted"], 1)

            def shift_mean(t, b):
                dve.wait_ge(s["inverted"], t * 2 + b + 1)
                nc.vector.scalar_tensor_tensor(out=shift[:, b, :], in0=mv[:, b, :, 0], scalar=-1.0, in1=rstd[:, b, :],
                                               op0=ALU.mult, op1=ALU.mult).then_inc(s["rstd_ready"], 1)

            def trip(t, b, first=False, last=False):
                i = t * 2 + b
                before = (t - 1 + b, 1 - b)
                dve.wait_ge(s["normed"], i + 1)
                for k in range(TT):
                    n = i * TT + k
                    if k % 4 == 0:
                        dve.wait_ge(s["h_made"], i * len(BANKS) + k // 4 + 1)
                    nc.vector.scalar_tensor_tensor(
                        out=Y[:, b, k, :], in0=h_ps[b][k], scalar=inv[:, bass.ds(n, 1)],
                        in1=base[:, bass.ds(n, 1), :].rearrange("p a f -> p (a f)"), op0=ALU.mult, op1=ALU.add).then_inc(s["z_ready"], 1)
                if not first:
                    invert(*before)
                dve.wait_ge(s["z_ready"], (i + 1) * TT)
                nc.vector.scalar_tensor_tensor(out=Y[:, b, :, :], in0=Y[:, b, :, :], scalar=0.0, in1=x_sb[:, bass.ds(i * TT, TT), :],
                                               op0=ALU.max, op1=ALU.add).then_inc(s["y_ready"], 1)
                if not first:
                    shift_mean(*before)
                dve.wait_ge(s["y_ready"], i + 3)
                for k in range(TT):
                    last_k = nc.vector.bn_stats(stats[:, k, :], Y[:, b, k, :])
                last_k.then_inc(s["stats_ready"], 1)
                if not last:
                    add_pair(t + 1, b)
                dve.wait_ge(s["stats_ready"], i + 1)
                dve.sem_inc(s["aggregating"], 1)
                for k in range(TT):
                    last_k = nc.vector.bn_aggr(mv[:, b, k, :], stats[:, k, :])
                last_k.then_inc(s["mv_ready"], 1)

            dve.wait_ge(s["rows_taken"], G + 1)
            for b in range(2):
                add_pair(0, b, first=True)
            for b in range(2):
                trip(0, b, first=b == 0)
            with dve.Fori(1, TG // 2 - 1) as t:
                for b in range(2):
                    trip(t, b)
            for b in range(2):
                trip(TG // 2 - 1, b, last=True)
            invert(TG // 2 - 1, 1)
            shift_mean(TG // 2 - 1, 1)

        @block.tensor
        def _(pe):
            idf, idb = ident[0:ROWS, 0:ROWS], ident_b[0:ROWS, 0:ROWS]
            pe.wait_ge(s["consts_set"], 4)

            def turn_dst(g):
                if g >= 2:
                    pe.wait_ge(s["key_taken"], g - 1)
                for j in range(TPG):
                    e = slice((g * TPG + j) * P, (g * TPG + j + 1) * P)
                    last = nc.tensor.matmul(cols_ps[g % 2][2][:, j, 0:ROWS], dst_f[:, e], idf, start=True, stop=True)
                last.then_inc(s["dst_turned"], 1)

            def turn_src(g):
                if g >= 2:
                    pe.wait_ge(s["src_taken"], 2 * (g - 1))
                for j in range(TPG):
                    e = slice((g * TPG + j) * P, (g * TPG + j + 1) * P)
                    nc.tensor.matmul(cols_ps[g % 2][0][:, j, 0:ROWS], src_hi[:, e], idb, start=True, stop=True)
                    last = nc.tensor.matmul(cols_ps[g % 2][1][:, j, 0:ROWS], src_lo[:, e], idb, start=True, stop=True)
                last.then_inc(s["src_turned"], 1)

            pe.wait_ge(s["dst_ready"], 1)
            turn_dst(0)
            pe.wait_ge(s["src_split"], 2)
            turn_src(0)
            turn_dst(1)
            turn_src(1)
            pe.wait_ge(s["low_spread"], 1)
            nc.tensor.matmul(b_x_flat[:, 0:GPR * ROWS], ones[0:ROWS, :], low_diag.rearrange("r g c -> r (g c)"),
                             start=True, stop=True).then_inc(s["low_turned"], 1)
            pe.wait_ge(s["rows_ready"], 1)
            nc.tensor.matmul(b_x[:, 0, 0:1], ones[0:ROWS, :], wide1[:, :], start=True, stop=True).then_inc(s["wide_summed"], 1)
            for g in range(2, GPR):
                turn_src(g)
                turn_dst(g)
            pe.wait_ge(s["wide_ready"], 1)

            def spread(r, g):
                one = ident_b[0:ROWS, bass.ds(r, 1)].to_broadcast([ROWS, P])
                e = slice(g * GE, (g + 1) * GE)
                o = b_src[g % 2][:, :, :].rearrange("p j e -> p (j e)")
                nc.tensor.matmul(o, one, src_hi[:, e], start=True, stop=False)
                nc.tensor.matmul(o, one, src_lo[:, e], start=False, stop=True).then_inc(s["src_spread"], 1)

            pe.wait_ge(s["src_taken"], 2 * GPR)
            spread(0, 0)
            pe.wait_ge(s["weights_loaded"], 96)
            nc.tensor.transpose(b_x[:, 0, :], w_lin_sb[:, :], ident[:, :])
            nc.tensor.transpose(b_x[:, 1, :], w_msg_sb[:, :], ident[:, :]).then_inc(s["wT_made"], 1)
            pe.wait_ge(s["wT_taken"], 1)
            pe.wait_ge(s["rows_ready"], 2)
            nc.tensor.matmul(b_x[:, 0, :], w_linT[:, :], wu_sb[:, 0, :], start=True, stop=True)
            nc.tensor.matmul(b_x[:, 1, :], w_msgT[:, :], wu_sb[:, 1, :], start=True, stop=True)
            nc.tensor.matmul(b_x[:, 2, :], b_msg_w[:, :], wu_sb[:, 1, :], start=True, stop=True)
            nc.tensor.matmul(b_x[0:1, 3, :], b_lin_c[:, :], wu_sb[:, 0, :], start=True, stop=False)
            nc.tensor.matmul(b_x[0:1, 3, :], ones[0:1, 0:1], b_upd_r[:, :], start=False, stop=True).then_inc(s["w_made"], 1)
            pe.wait_ge(s["w_taken"], 1)
            nc.tensor.matmul(hist, zeros_b[:, :], zeros_b[:, 0:NT], start=True, stop=False)
            is_wide = nc.tensor.value_load(wide_i[0:1, 0:1], min_val=0, max_val=1)
            pe.sem_inc(s["rows_made"], WS)

            def edge_loop(gathered, phase):
                with pe.Fori(*PHASES[phase]) as r:
                    for g in range(GPR):
                        i = r * GPR + g
                        b = g % 2
                        pe.wait_ge(s["before_ready"], i + 1)
                        pe.wait_ge(s["dup_taken"], i + 1)
                        for j in range(TPG):
                            last = nc.tensor.matmul(b_dup[:, j:j + 1], eq_before[:, b, j, :], one_b[:, :], start=True, stop=True)
                        last.then_inc(s["dup_made"], 1)
                        pe.wait_ge(s["key_hot"], i + 1)
                        for j in range(TPG):
                            last = nc.tensor.matmul(b_M[:, j, :], hot_key[:, b, j, :], eq[:, b, j, :], start=True, stop=True)
                        last.then_inc(s["M_made"], 1)
                        spread(r if g < GPR - 1 else r + 1, (g + 1) % GPR)
                        if phase < 2:
                            pe.wait_ge(s["hi_hot"], i + 1)
                            for j in range(TPG):
                                nc.tensor.matmul(hist, hot_lo[:, b, j, :], hot_hi[:, b, j, :], start=False, stop=False)
                        if phase == 0 and g < MORE_HIST:
                            pe.wait_ge(s["more_hi_hot"], r * MORE_HIST + g + 1)
                            for j in range(TPG):
                                nc.tensor.matmul(hist, more_lo[b][:, j, :], more_hi[b][:, j, :], start=False, stop=False)
                        if gathered:
                            pe.wait_ge(win_gathered[g], (r + 1) * 16 * TPG)
                        else:
                            pe.wait_ge(win_loaded[g], (r + 1) * 16)
                        pe.wait_ge(s["M_taken"], i + 1)
                        pe.wait_ge(s["rows_taken"], i + 1)
                        for j in range(TPG):
                            last = nc.tensor.matmul(b_rows[:, j, :], M[:, b, j, :], win[:, g, j if gathered else 0, :], start=True, stop=True)
                        last.then_inc(s["rows_made"], 1)
                        if g == 1:
                            pe.wait_ge(s["x_copied"], r + 2)
                            nc.tensor.transpose(b_x[:, 0, :], x_now[:, :], ident[:, :]).then_inc(s["x_turned"], 1)
                        if g == 2:
                            pe.wait_ge(s["xT_taken"], r + 1)
                            nc.tensor.matmul(b_x[:, 1, :], xT[:, :], A[:, :], start=True, stop=False)
                            nc.tensor.matmul(b_x[:, 1, :], ones[0:1, :], const_row[:, :], start=False, stop=True).then_inc(s["base_made"], 1)

            def edge_loops(gathered):
                edge_loop(gathered, 0)
                edge_loop(gathered, 1)
                nc.tensor.matmul(hist, zeros_b[:, :], zeros_b[:, 0:NT], start=False, stop=True).then_inc(s["hist_final"], 1)
                edge_loop(gathered, 2)

            with pe.If(is_wide == 0):
                edge_loops(False)
            with pe.Else():
                edge_loops(True)
            with pe.Fori(0, TG // 2) as t:
                for b in range(2):
                    i = t * 2 + b
                    pe.wait_ge(s["S_summed"], i + 1)
                    for q, tiles in enumerate(BANKS):
                        for k in tiles:
                            last = nc.tensor.transpose(b_src[q][:, k - tiles.start, :], S_all[:, b, k, :], ident[:, :])
                        last.then_inc(s["S_turned"], 1)
                    pe.wait_ge(s["y_ready"], i + 1)
                    for q, tiles in enumerate(BANKS):
                        pe.wait_ge(s["ST_taken"], i * len(BANKS) + q + 1)
                        for k in tiles:
                            last = nc.tensor.matmul(h_ps[b][k], ST[:, k, :], B[:, :], start=True, stop=True)
                        last.then_inc(s["h_made"], 1)


_INS = ["x", "src", "dst", "L0_gnn_W_lin", "L0_gnn_b_lin", "L0_gnn_W_msg", "L0_gnn_b_msg", "L0_gnn_W_upd", "L0_gnn_b_upd"]


def kernel(**inputs):
    import concourse.bacc as bacc
    from concourse.bass_utils import run_bass_kernel_spmd

    nc = bacc.Bacc("TRN2", target_bir_lowering=False, num_devices=1)
    arrays, args = {}, []
    for name in _INS:
        a = np.ascontiguousarray(inputs[name])
        arrays[f"in_{name}"] = a
        args.append(nc.dram_tensor(f"in_{name}", a.shape, mybir.dt.from_np(a.dtype), kind="ExternalInput").ap())
    shape = arrays["in_x"].shape
    out = nc.dram_tensor("out_0", shape, mybir.dt.float32, kind="ExternalOutput").ap()
    gnn_program(nc, *args, out)
    r = run_bass_kernel_spmd(nc, [arrays], core_ids=[0])
    return r.results[0]["out_0"]
```
